# Optimizing a Trainium2 kernel written in Bass

```python
import numpy as np
import jax
import jax.numpy as jnp

def _softmax(x, axis=-1):
    return jax.nn.softmax(x, axis=axis)

def _gelu(x):
    return jax.nn.gelu(x, approximate=True)

def _silu(x):
    return jax.nn.silu(x)

def _sigmoid(x):
    return jax.nn.sigmoid(x)

def _layernorm(x, axis=-1, eps=1e-05):
    m = jnp.mean(x, axis=axis, keepdims=True)
    v = jnp.var(x, axis=axis, keepdims=True)
    return (x - m) / jnp.sqrt(v + eps)

def _scatter_add(tgt, idx, src, axis=0):
    return tgt.at[idx].add(src)

def _segment_sum(src, seg, n):
    return jax.ops.segment_sum(src, seg, n)
kernel_name = 'mk_recurrent_d1_jaxref_r4_74767a'

def setup_inputs(seed: int=0):
    np.random.seed(seed)
    _w = jnp.asarray

    def _L0_attn_setup():
        import jax, jax.numpy as jnp
        import numpy as np
        H = 1024
        D_IN = 2048
        N = 16
        K = 4
        R = 64
        EPS = 1e-06

        def rms_forward(x, eps=EPS):
            xf = x.astype(jnp.float32)
            var = jnp.mean(xf * xf, axis=-1, keepdims=True)
            return (xf * jax.lax.rsqrt(var + eps)).astype(x.dtype)
        key = jax.random.key(seed)
        ks = jax.random.split(key, 10)
        s = 0.02
        hidden_states = jax.random.normal(ks[0], (2, 256, H), dtype=jnp.float32)
        W_in = jax.random.normal(ks[1], (2 * D_IN, H), dtype=jnp.float32) * s
        conv_w = jax.random.normal(ks[2], (D_IN, K), dtype=jnp.float32) * 0.2
        conv_b = jax.random.normal(ks[3], (D_IN,), dtype=jnp.float32) * 0.02
        W_x = jax.random.normal(ks[4], (R + 2 * N, D_IN), dtype=jnp.float32) * s
        W_dt = jax.random.normal(ks[5], (D_IN, R), dtype=jnp.float32) * s
        b_dt = jax.random.normal(ks[6], (D_IN,), dtype=jnp.float32) * 0.02
        A_log = jnp.log(jnp.broadcast_to(jnp.arange(1, N + 1, dtype=jnp.float32)[None, :], (D_IN, N)))
        D = jnp.ones((D_IN,), dtype=jnp.float32)
        W_out = jax.random.normal(ks[7], (H, D_IN), dtype=jnp.float32) * s
        return {'hidden_states': hidden_states, 'W_in': W_in, 'conv_w': conv_w, 'conv_b': conv_b, 'W_x': W_x, 'W_dt': W_dt, 'b_dt': b_dt, 'A_log': A_log, 'D': D, 'W_out': W_out}
    _L0_attn_in = _L0_attn_setup()

    def _L0_ffn_setup():
        import jax, jax.numpy as jnp
        import numpy as np
        NUM_EXPERTS = 8
        RANK = 32
        ALPHA = 16.0
        TOP_K = 2
        TEMPERATURE = 1.0
        GAMMA = 0.5
        SOFT_TOPK_TEMP = 0.5
        N_GRAM = 2
        EPS = 1e-06
        key = jax.random.key(seed)
        ks = jax.random.split(key, 6)
        d_in, d_out = (1024, 1024)
        Bsz, T = (4, 512)
        x = jax.random.normal(ks[0], (Bsz, T, d_in), dtype=jnp.float32)
        W = jax.random.normal(ks[1], (d_out, d_in), dtype=jnp.float32) / np.sqrt(d_in)
        b = jax.random.normal(ks[2], (d_out,), dtype=jnp.float32) * 0.01
        A = jax.random.normal(ks[3], (d_in, RANK), dtype=jnp.float32) / np.sqrt(d_in)
        Bmat = jax.random.normal(ks[4], (RANK, d_out), dtype=jnp.float32) * 0.01
        LiMEs = jax.random.normal(ks[5], (NUM_EXPERTS, RANK), dtype=jnp.float32) * 0.1
        return {'x': x, 'W': W, 'b': b, 'A': A, 'Bmat': Bmat, 'LiMEs': LiMEs}
    _L0_ffn_in = _L0_ffn_setup()
    _d = {'L0_attn_hidden_states': _L0_attn_in['hidden_states'], 'L0_attn_W_in': _L0_attn_in['W_in'], 'L0_attn_conv_w': _L0_attn_in['conv_w'], 'L0_attn_conv_b': _L0_attn_in['conv_b'], 'L0_attn_W_x': _L0_attn_in['W_x'], 'L0_attn_W_dt': _L0_attn_in['W_dt'], 'L0_attn_b_dt': _L0_attn_in['b_dt'], 'L0_attn_A_log': _L0_attn_in['A_log'], 'L0_attn_D': _L0_attn_in['D'], 'L0_attn_W_out': _L0_attn_in['W_out'], 'L0_ffn_W': _L0_ffn_in['W'], 'L0_ffn_b': _L0_ffn_in['b'], 'L0_ffn_A': _L0_ffn_in['A'], 'L0_ffn_Bmat': _L0_ffn_in['Bmat'], 'L0_ffn_LiMEs': _L0_ffn_in['LiMEs']}
    _x0 = _d['L0_attn_hidden_states']
    _d['L0_attn_hidden_states'] = jax.random.normal(jax.random.fold_in(jax.random.key(seed), 1), (2, 1024, 1024), dtype=_x0.dtype)
    del _x0
    return _d

def reference(L0_attn_hidden_states, L0_attn_W_in, L0_attn_conv_w, L0_attn_conv_b, L0_attn_W_x, L0_attn_W_dt, L0_attn_b_dt, L0_attn_A_log, L0_attn_D, L0_attn_W_out, L0_ffn_W, L0_ffn_b, L0_ffn_A, L0_ffn_Bmat, L0_ffn_LiMEs):

    def _L0_attn_ref(hidden_states, W_in, conv_w, conv_b, W_x, W_dt, b_dt, A_log, D, W_out):
        import jax, jax.numpy as jnp
        import numpy as np
        H = 1024
        D_IN = 2048
        N = 16
        K = 4
        R = 64
        EPS = 1e-06

        def rms_forward(x, eps=EPS):
            xf = x.astype(jnp.float32)
            var = jnp.mean(xf * xf, axis=-1, keepdims=True)
            return (xf * jax.lax.rsqrt(var + eps)).astype(x.dtype)
        b, L, _ = hidden_states.shape
        proj = hidden_states @ W_in.T
        x, gate = (proj[..., :D_IN], proj[..., D_IN:])
        xpad = jnp.pad(x, ((0, 0), (K - 1, 0), (0, 0)))
        xc = conv_b
        for j in range(K):
            xc = xc + conv_w[:, j] * xpad[:, j:j + L, :]
        x = jax.nn.silu(xc)
        ssm = x @ W_x.T
        ts, Bm, Cm = (ssm[..., :R], ssm[..., R:R + N], ssm[..., R + N:])
        ts = rms_forward(ts)
        Bm = rms_forward(Bm)
        Cm = rms_forward(Cm)
        dt = jax.nn.softplus(ts @ W_dt.T + b_dt)
        A = -jnp.exp(A_log.astype(jnp.float32))

        def step(state, inp):
            dt_t, B_t, C_t, u_t = inp
            dA = jnp.exp(dt_t[..., None] * A)
            state = state * dA + (dt_t * u_t)[..., None] * B_t[:, None, :]
            y = jnp.einsum('bdn,bn->bd', state, C_t)
            return (state, y)
        init = jnp.zeros((b, D_IN, N), dtype=jnp.float32)
        xs = (dt.transpose(1, 0, 2), Bm.transpose(1, 0, 2), Cm.transpose(1, 0, 2), x.transpose(1, 0, 2))
        _, ys = jax.lax.scan(step, init, xs)
        y = ys.transpose(1, 0, 2) + x * D
        y = y * jax.nn.silu(gate)
        return y @ W_out.T

    def _L0_ffn_ref(x, W, b, A, Bmat, LiMEs):
        import jax, jax.numpy as jnp
        import numpy as np
        NUM_EXPERTS = 8
        RANK = 32
        ALPHA = 16.0
        TOP_K = 2
        TEMPERATURE = 1.0
        GAMMA = 0.5
        SOFT_TOPK_TEMP = 0.5
        N_GRAM = 2
        EPS = 1e-06
        Bsz, T, d_in = x.shape
        E = LiMEs.shape[0]
        scaling = ALPHA / RANK
        H = jnp.einsum('btd,od->bto', x, W) + b
        z = jnp.einsum('btd,dr->btr', x, A)
        anchors = jnp.arange(N_GRAM - 1, T, N_GRAM)
        H_slice = H[:, anchors, :E]
        delta_slice = jnp.einsum('bar,er->bae', z[:, anchors], LiMEs)
        H_scale = jnp.maximum(jnp.max(jnp.abs(H_slice)), EPS)
        d_scale = jnp.maximum(jnp.max(jnp.abs(delta_slice)), EPS)
        logits = ((1.0 - GAMMA) * (H_slice / H_scale) + GAMMA * (delta_slice / d_scale)) / TEMPERATURE
        probs = jax.nn.softmax(logits, axis=-1)
        topk_vals, _ = jax.lax.top_k(probs, TOP_K)
        thresh = topk_vals[..., -1:]
        mask = jax.nn.sigmoid((probs - thresh) / SOFT_TOPK_TEMP)
        weights = probs * mask
        weights = weights / (jnp.sum(weights, axis=-1, keepdims=True) + 1e-09)
        weights_full = jnp.repeat(weights, N_GRAM, axis=1)
        p_mix = jnp.einsum('bte,er->btr', weights_full, LiMEs)
        delta = jnp.einsum('btr,ro->bto', z * p_mix, Bmat) * scaling
        return H + delta
    x = L0_attn_hidden_states
    xn = _layernorm(x, axis=-1)
    s = _L0_attn_ref(xn, L0_attn_W_in, L0_attn_conv_w, L0_attn_conv_b, L0_attn_W_x, L0_attn_W_dt, L0_attn_b_dt, L0_attn_A_log, L0_attn_D, L0_attn_W_out)
    g = _silu(_L0_ffn_ref(xn, L0_ffn_W, L0_ffn_b, L0_ffn_A, L0_ffn_Bmat, L0_ffn_LiMEs))
    x = x + s * g
    return x

_drawn_inputs = setup_inputs


def setup_inputs(seed=0):
    import zlib

    import numpy as np

    out = dict(_drawn_inputs(seed))
    spreads = {'L0_attn_D': (1.0, 0.6)}
    factors = {'L0_attn_conv_b': 4.031,
     'L0_attn_W_dt': 3.319,
     'L0_attn_b_dt': 25.058,
     'L0_ffn_b': 45.732,
     'L0_ffn_A': 8.0,
     'L0_ffn_Bmat': 8.0,
     'L0_ffn_LiMEs': 8.0}
    for name, (base, spread) in spreads.items():
        noise = np.random.default_rng([zlib.crc32(name.encode()), seed]).standard_normal(out[name].shape)
        drawn = base * np.exp(spread * noise) if base else spread * noise
        out[name] = jnp.asarray(drawn.astype(out[name].dtype))
    for name, factor in factors.items():
        out[name] = (out[name] * factor).astype(out[name].dtype)
    return out
```

```python
from contextlib import ExitStack

import concourse.bass as bass
from concourse import mybir

F32 = mybir.dt.float32
ALU = mybir.AluOpType
ACT = mybir.ActivationFunctionType
AX = mybir.AxisListType

P = 128
BATCH, L, H = 2, 1024, 1024
D_IN, N, K_CONV, R = 2048, 16, 4, 64
E, RANK = 8, 32
TOK = BATCH * L
T = 512
NC = TOK // T
HALVES = L // T
KH = H // P
MT = D_IN // P
OT = H // P
SS = R + 2 * N
TT = TOK // P
NA = P // 2
U = 2
NU = N // U
PAIRS = MT // 2
WX = KH * P
WXX = WX + SS
WXW = WXX + K_CONV + 1
SP_A, SP_B, SP_D, SP_W = 0, N, N + 1, N + 2
SPW = SP_W + P
FW = KH * P + P + 1
HALO = K_CONV - 1


class Seq:

    def __init__(self, eng, sem):
        self.eng, self.sem, self.base, self.turn, self.n = eng, sem, 0, 0, 0

    def start(self, per, turn):
        self.per, self.turn, self.n = per, turn, 0

    def end(self, turns):
        assert self.n == self.per, (self.n, self.per)
        self.base += self.per * turns

    def did(self, ins):
        ins.then_inc(self.sem, 1)
        self.n += 1

    def wait(self):
        self.eng.wait_ge(self.sem, self.turn * self.per + (self.base + self.n))


def build(nc, x, xt, w_in, w_s, w_g, w_o, w_f, w8, a_r, lime, lime_t, b8, ident, blk, out):
    ctx = ExitStack()
    with ctx:
        sb = lambda name, shape: ctx.enter_context(nc.sbuf_tensor(name, shape, F32))
        sem = lambda name: ctx.enter_context(nc.semaphore(name))
        dram = lambda name, shape: nc.dram_tensor(name, shape, F32, kind="Internal").ap()

        xn_d = dram("xn_d", (TT, P, KH, P))
        zp_d = dram("zp_d", (NC, RANK, T))
        u_d = dram("u_d", (NC, MT, P, T))
        sg_d = dram("sg_d", (NC, MT, P, T))
        g_d = dram("g_d", (NC, OT, P, T))
        y_d = dram("y_d", (NC, MT, P, T))
        bc_d = dram("bc_d", (NC, 2, N * T))

        idt = sb("idt", [P, P])
        blkt = sb("blkt", [SS, SS])
        eps = sb("eps", [P, 3])
        bb = sb("bb", [P, N, T])
        cb = sb("cb", [P, N, T])
        hb = sb("hb", [P, 2, U, T])
        da = sb("da", [P, 2, U, T])
        yb = sb("yb", [P, MT, T])
        xn = sb("xn", [P, KH, T])
        zp = sb("zp", [RANK, T])
        wx = sb("wx", [P, 2, WXW])
        wg = sb("wg", [P, 2, WX])
        wf = sb("wf", [P, FW])
        wo = sb("wo", [P, MT * P])
        ws = sb("ws", [P, 2, SPW])
        xraw = sb("xraw", [P, T + HALO])
        tails = sb("tails", [P, MT, HALO])
        xc = sb("xc", [P, T])
        uo = sb("uo", [P, 2, T])
        sgo = sb("sgo", [P, T])
        fo = sb("fo", [P, T])
        ui = sb("ui", [P, 2, T])
        sgi = sb("sgi", [P, 2, T])
        rl = sb("rl", [P, T])
        lg = sb("lg", [P, T])
        ndt = sb("ndt", [P, T])
        dtu = sb("dtu", [P, T])
        aex = sb("aex", [P, 2, N])
        st = sb("st", [P, N])
        states = sb("states", [P, MT, N])
        yacc = sb("yacc", [P, T])
        yo = sb("yo", [P, T])
        xo = sb("xo", [P, T])
        go = sb("go", [P, T])
        ssr = sb("ssr", [SS, T])
        ssn = sb("ssn", [SS, T])
        ps = [ctx.enter_context(nc.psum_tensor(f"ps{k}", [P, T], F32)) for k in range(8)]
        p_x, p_g, p_dt, p_ss, p_o, p_f, p_ms, _ = ps

        flat = lambda t: t[:].rearrange("p a b -> p (a b)")
        lnx = [bb[:, 2 * j:2 * j + 2, :].rearrange("p a b -> p (a b)") for j in range(2)]
        lnn = [bb[:, 4 + 2 * j:6 + 2 * j, :].rearrange("p a b -> p (a b)") for j in range(2)]
        lnt = [bb[:, 8 + 2 * j:10 + 2 * j, :].rearrange("p a b -> p (a b)").rearrange("p (k t) -> p k t", k=KH) for j in range(2)]
        z_t = cb[0:RANK, 0:TOK // T, :].rearrange("p a b -> p (a b)")
        w8t = cb[:, 4, 0:KH * E].rearrange("p (k e) -> p k e", k=KH)
        art = cb[:, 5, 0:KH * RANK].rearrange("p (k e) -> p k e", k=KH)
        limet = cb[0:E, 6, 0:RANK]
        limett = cb[0:RANK, 6, RANK:RANK + E]
        b8t = cb[0:NA, 7, 0:E]
        w_t = cb[0:E, 8:10, :].rearrange("p a b -> p (a b)")
        rt = lambda k: cb[0:NA, 10 + k // 4, (k % 4) * TT * E:(k % 4 + 1) * TT * E].rearrange("p (a b) -> p a b", a=TT)
        small = cb[:, 14, :]
        st6 = small[:, 0:24].rearrange("p (j a b) -> p j a b", j=2, a=2)
        mv = small[:, 24:28].rearrange("p (j a) -> p j a", j=2)
        std = small[:, 28:32]
        gmx = small[0:NA, 40:48]
        r16 = lambda k: small[0:NA, 64 + 16 * k:80 + 16 * k]

        s_const, s_eps = sem("s_const"), sem("s_eps")
        ln_in = [sem("ln_in0"), sem("ln_in1")]
        ln_var, ln_std, ln_norm = sem("ln_var"), sem("ln_std"), sem("ln_norm")
        ln_tr, ln_tc, ln_zh = sem("ln_tr"), sem("ln_tc"), sem("ln_zh")
        ln_z, ln_h, ln_st = sem("ln_z"), sem("ln_h"), sem("ln_st")
        r_pe, r_act, r_dve, r_pool, r_zp = sem("r_pe"), sem("r_act"), sem("r_dve"), sem("r_pool"), sem("r_zp")
        ld_x = [sem("ld_x0"), sem("ld_x1")]
        ld_g = [sem("ld_g0"), sem("ld_g1")]
        ld_s = [sem("ld_s0"), sem("ld_s1")]
        ld_f, ld_o, ld_xn, ld_y, ld_b, ld_c = (sem(n) for n in ("ld_f", "ld_o", "ld_xn", "ld_y", "ld_b", "ld_c"))
        st_u, st_sg, st_g, st_y, st_o, st_bc = (sem(n) for n in ("st_u", "st_sg", "st_g", "st_y", "st_o", "st_bc"))
        pe_x, act_x, dve_conv, act_u, pe_ss = (sem(n) for n in ("pe_x", "act_x", "dve_conv", "act_u", "pe_ss"))
        pe_g, act_sg, pe_f, act_f = (sem(n) for n in ("pe_g", "act_sg", "pe_f", "act_f"))
        act_ss, pe_ms, act_rms, dve_ssn = (sem(n) for n in ("act_ss", "pe_ms", "act_rms", "dve_ssn"))
        pe_dt, act_sp, dve_dt, act_da, dve_h, pool_p, dve_y = (
            sem(n) for n in ("pe_dt", "act_sp", "dve_dt", "act_da", "dve_h", "pool_p", "dve_y"))
        pe_o, dve_o = sem("pe_o"), sem("dve_o")
        sp_passed, dve_passed = sem("sp_passed"), sem("dve_passed")
        act_seq, dve_seq = sem("act_seq"), sem("dve_seq")

        block = ctx.enter_context(nc.Block())

        def slots():
            for s in range(NC + 2):
                chunk = lambda c: c if 0 <= c < NC else None
                yield chunk(s), chunk(s - 1), chunk(s - 2)

        def pairs(eng, body):
            body(0, True, False, 1)
            with eng.Fori(1, PAIRS - 1) as i:
                body(i, False, False, PAIRS - 2)
            body(PAIRS - 1, False, True, 1)

        @block.sync
        def _(sp):
            def wait(s, count):
                sp.wait_ge(s, count)
                if not isinstance(count, int):
                    sp.sem_inc(sp_passed, 1)

            for dst, src in ((idt[:], ident), (blkt[:], blk), (w8t, w8), (art, a_r), (limet, lime),
                             (limett, lime_t), (b8t, b8)):
                sp.dma_start(dst, src).then_inc(s_const, 16)

            def ln_load(t, j, pair):
                sp.dma_start(lnx[j], x[t]).then_inc(ln_in[j], 16)

            ln_load(0, 0, 0)
            ln_load(1, 1, 0)
            def ln_pair(i):
                for j in range(2):
                    t = i * 2 + j
                    wait(ln_norm, t + 1)
                    wait(ln_tc, t + 1)
                    sp.dma_start(xn_d[t], lnt[j]).then_inc(ln_st, 16)
                    nxt = t + 2
                    sp.dma_start(lnx[j], x[nxt]).then_inc(ln_in[j], 16)

            ln_pair(0)
            with sp.Fori(1, TT // 2) as i:
                ln_pair(i)
            wait(ln_in[0], 16 * (TT // 2 + 1))
            wait(ln_in[1], 16 * (TT // 2 + 1))
            wait(ln_st, 16 * TT)
            wait(r_zp, 1)
            for c in range(NC):
                sp.dma_start(zp_d[c], z_t[:, c * T:(c + 1) * T]).then_inc(ln_st, 16)
            wait(ln_st, 16 * (TT + NC))

            def load_x(c, m, j, gx):
                sp.dma_start(wx[:, j, :], w_in[m]).then_inc(ld_x[j], 16)
                sp.dma_start(wg[:, j, :], w_g[m]).then_inc(ld_g[j], 16)

            def load_s(c, m, j):
                sp.dma_start(ws[:, j, :], w_s[m]).then_inc(ld_s[j], 16)
                sp.dma_start(ui[:, j, :], u_d[c, m]).then_inc(ld_s[j], 16)
                sp.dma_start(sgi[:, j, :], sg_d[c, m]).then_inc(ld_s[j], 16)

            for cx, cs, co in slots():
                if cx is not None:
                    if cx > 0:
                        wait(pe_g, MT * cx)
                        wait(pe_f, OT * cx)
                        wait(pe_ss, MT * cx)
                        wait(dve_conv, MT * cx)
                        wait(act_f, OT * cx)
                    load_x(cx, 0, 0, MT * cx)
                    sp.dma_start(wf[:], w_f[0]).then_inc(ld_f, 16)
                    for r in range(T // P):
                        sp.dma_start(xn[:, :, r * P:(r + 1) * P], xn_d[cx * (T // P) + r]).then_inc(ld_xn, 16)
                    sp.dma_start(zp[:], zp_d[cx]).then_inc(ld_xn, 16)
                if cs is not None:
                    wait(st_u, 16 * MT * (cs + 1))
                    wait(st_sg, 16 * MT * (cs + 1))
                    if cs > 0:
                        wait(dve_y, MT * cs)
                    load_s(cs, 0, 0)
                    wait(dve_ssn, cs + 1)
                    sp.dma_start(bc_d[cs].rearrange("a (n t) -> (a n) t", n=N), ssn[R:SS, :]).then_inc(st_bc, 16)
                    wait(st_bc, 16 * (cs + 1))
                    if cs > 0:
                        wait(pool_p, NU * MT * cs)
                    for h4 in range(2):
                        w = N * T // 2
                        sp.dma_start(flat(bb)[:, h4 * w:(h4 + 1) * w],
                                     bc_d[cs, 0:1, h4 * w:(h4 + 1) * w].partition_broadcast(P)).then_inc(ld_b, 16)
                        sp.dma_start(flat(cb)[:, h4 * w:(h4 + 1) * w],
                                     bc_d[cs, 1:2, h4 * w:(h4 + 1) * w].partition_broadcast(P)).then_inc(ld_c, 16)
                if co is not None:
                    wait(st_y, 16 * MT * (co + 1))
                    wait(st_g, 16 * OT * (co + 1))
                    if co > 0:
                        wait(pe_o, OT * co)
                    sp.dma_start(yb[:], y_d[co].rearrange("m p t -> p m t")).then_inc(ld_y, 16)

                def body(i, first, last, turns, cx=cx, cs=cs, co=co):
                    for j in range(2):
                        m = i * 2 + j
                        if not (last and j == 1):
                            nj = 1 - j
                            if cs is not None:
                                gs = m + MT * cs
                                if cs > 0 or not (first and j == 0):
                                    wait(dve_y, gs)
                                load_s(cs, m + 1, nj)
                            if cx is not None:
                                gx = m + MT * cx
                                if cx > 0 or not (first and j == 0):
                                    wait(pe_ss, gx)
                                    wait(pe_g, gx)
                                    wait(dve_conv, gx)
                                load_x(cx, m + 1, nj, gx + 1)
                        if cx is not None:
                            gx = m + MT * cx
                            wait(act_u, gx + 1)
                            sp.dma_start(u_d[cx, m], uo[:, j, :]).then_inc(st_u, 16)
                            wait(act_sg, gx + 1)
                            sp.dma_start(sg_d[cx, m], sgo[:]).then_inc(st_sg, 16)
                            if j == 0:
                                gf = i + OT * cx
                                wait(act_f, gf + 1)
                                sp.dma_start(g_d[cx, i], fo[:]).then_inc(st_g, 16)
                                if not last:
                                    sp.dma_start(wf[:], w_f[i + 1]).then_inc(ld_f, 16)
                        if co is not None:
                            go_n = i + OT * co
                            if j == 0:
                                if co > 0 or not first:
                                    wait(pe_o, go_n)
                                    wait(dve_o, go_n)
                                    wait(st_o, 16 * go_n)
                                sp.dma_start(wo[:], w_o[i]).then_inc(ld_o, 16)
                                sp.dma_start(xo[:], xt[co, i]).then_inc(ld_o, 16)
                                sp.dma_start(go[:], g_d[co, i]).then_inc(ld_o, 16)
                            else:
                                wait(dve_o, go_n + 1)
                                sp.dma_start(out[co, i], xo[:]).then_inc(st_o, 16)
                        if cs is not None:
                            gs = m + MT * cs
                            wait(dve_y, gs + 1)
                            sp.dma_start(y_d[cs, m], yo[:]).then_inc(st_y, 16)

                pairs(sp, body)
            sp.wait_ge(st_o, 16 * OT * NC)

        @block.tensor
        def _(pe):
            mm = nc.tensor.matmul

            pe.wait_ge(s_const, 16 * 7)
            def ln_pair(i):
                for j in range(2):
                    t = i * 2 + j
                    pe.wait_ge(ln_norm, t + 1)
                    for k in range(KH):
                        ins = nc.tensor.transpose(ps[2 * j + k // 4][:, (k % 4) * P:(k % 4 + 1) * P],
                                                  lnn[j][:, k * P:(k + 1) * P], idt[:])
                    ins.then_inc(ln_tr, 1)
                    pe.wait_ge(ln_tc, t + 1)
                    if not (isinstance(i, int) and j == 0):
                        pe.wait_ge(ln_z, t)
                        pe.wait_ge(ln_h, t)
                    for k in range(KH):
                        mm(ps[4][0:RANK, 0:P], art[:, k, :], lnt[j][:, k, :], start=(k == 0), stop=(k == KH - 1))
                    for k in range(KH):
                        ins = mm(ps[5][0:NA, 0:E], lnt[j][:, k, 1:P:2], w8t[:, k, :], start=(k == 0), stop=(k == KH - 1))
                    ins.then_inc(ln_zh, 1)


            ln_pair(0)
            with pe.Fori(1, TT // 2) as i:
                ln_pair(i)
            pe.wait_ge(ln_z, TT)
            for t in range(TT):
                ins = mm(ps[6][0:NA, t * E:(t + 1) * E], z_t[:, t * P + 1:(t + 1) * P:2], limett, start=True, stop=True)
            ins.then_inc(r_pe, 1)
            pe.wait_ge(r_dve, 10)
            for t in range(TT):
                ins = nc.tensor.transpose(ps[t // 8][0:E, (t % 8) * NA:(t % 8 + 1) * NA], rt(5)[:, t, :], idt[0:NA, 0:NA])
            ins.then_inc(r_pe, 1)
            pe.wait_ge(r_act, 4)
            for h in range(2):
                ins = mm(ps[2 + h][0:RANK, :], limet, w_t[:, h * T:(h + 1) * T], start=True, stop=True)
            ins.then_inc(r_pe, 1)

            for cx, cs, co in slots():
                if cx is not None:
                    pe.wait_ge(ld_xn, 16 * (T // P + 1) * (cx + 1))
                if cx == 0:
                    pe.wait_ge(r_zp, 1)

                def dt_product(i, j, cs=cs):
                    gs = i * 2 + (j + MT * cs)
                    pe.wait_ge(ld_s[j], (i + PAIRS * cs + 1) * 48)
                    if not (cs == 0 and isinstance(i, int) and i == 0 and j == 0):
                        pe.wait_ge(act_sp, gs)
                    mm(p_dt[:], ws[0:R, j, SP_W:SPW], ssn[0:R, :], start=True, stop=True).then_inc(pe_dt, 1)

                if cs is not None:
                    pe.wait_ge(dve_ssn, cs + 1)
                    dt_product(0, 0)
                if co is not None:
                    pe.wait_ge(ld_y, 16 * (co + 1))

                def body(i, first, last, turns, cx=cx, cs=cs, co=co):
                    for j in range(2):
                        if cs is not None and not (last and j == 1):
                            dt_product(i + (1 if j == 1 else 0), 1 - j)
                        if cx is not None:
                            gx = i * 2 + (j + MT * cx)
                            pair = i + PAIRS * cx
                            start = cx == 0 and first and j == 0
                            pe.wait_ge(ld_x[j], (pair + 1) * 16)
                            if not start:
                                pe.wait_ge(act_x, gx)
                            for k in range(KH):
                                ins = mm(p_x[:], wx[:, j, k * P:(k + 1) * P], xn[:, k, :], start=(k == 0), stop=(k == KH - 1))
                            ins.then_inc(pe_x, 1)
                            if not (first and j == 0):
                                pe.wait_ge(act_u, gx)
                                if first and j == 1 and cx > 0:
                                    pe.wait_ge(act_ss, cx)
                                mm(p_ss[0:SS, :], wx[:, 1 - j, WX:WXX], uo[:, 1 - j, :],
                                   start=(first and j == 1), stop=False).then_inc(pe_ss, 1)
                            pe.wait_ge(ld_g[j], (pair + 1) * 16)
                            if not start:
                                pe.wait_ge(act_sg, gx)
                            for k in range(KH):
                                ins = mm(p_g[:], wg[:, j, k * P:(k + 1) * P], xn[:, k, :], start=(k == 0), stop=(k == KH - 1))
                            ins.then_inc(pe_g, 1)
                            if j == 0:
                                gf = i + OT * cx
                                pe.wait_ge(ld_f, (gf + 1) * 16)
                                if not start:
                                    pe.wait_ge(act_f, gf)
                                for k in range(KH):
                                    mm(p_f[:], wf[:, k * P:(k + 1) * P], xn[:, k, :], start=(k == 0), stop=False)
                                mm(p_f[:], wf[0:RANK, KH * P:KH * P + P], zp[:], start=False, stop=True).then_inc(pe_f, 1)
                        if co is not None and j == 1:
                            go_n = i + OT * co
                            pe.wait_ge(ld_o, (go_n + 1) * 48)
                            if not (co == 0 and first):
                                pe.wait_ge(dve_o, go_n)
                            for k in range(MT):
                                ins = mm(p_o[:], wo[:, k * P:(k + 1) * P], yb[:, k, :], start=(k == 0), stop=(k == MT - 1))
                            ins.then_inc(pe_o, 1)

                pairs(pe, body)
                if cx is not None:
                    pe.wait_ge(act_u, MT * (cx + 1))
                    mm(p_ss[0:SS, :], wx[:, 1, WX:WXX], uo[:, 1, :], start=False, stop=True).then_inc(pe_ss, 1)
                    pe.wait_ge(act_ss, cx + 1)
                    mm(p_ms[0:SS, :], blkt[:], ssn[:], start=True, stop=True).then_inc(pe_ms, 1)

        @block.scalar
        def _(act):
            seq = Seq(act, act_seq)
            f = nc.scalar.activation
            act.wait_ge(s_eps, 1)
            def ln_pair(i):
                for j in range(2):
                    t = i * 2 + j
                    act.wait_ge(ln_var, t + 1)
                    f(std[:, j:j + 1], mv[:, j, 1:2], ACT.Sqrt, bias=eps[:, 0:1]).then_inc(ln_std, 1)
                    act.wait_ge(ln_tr, t + 1)
                    if not (isinstance(i, int) and j == 0):
                        act.wait_ge(ln_st, t * 16)
                    for h in range(2):
                        ins = nc.scalar.copy(lnt[j][:, 4 * h:4 * h + 4, :], ps[2 * j + h][:].rearrange("p (a b) -> p a b", a=4))
                    ins.then_inc(ln_tc, 1)
                    act.wait_ge(ln_zh, t + 1)
                    nc.scalar.copy(z_t[:, bass.ds(t * P, P)], ps[4][0:RANK, 0:P]).then_inc(ln_z, 1)

            ln_pair(0)
            with act.Fori(1, TT // 2) as i:
                ln_pair(i)
            act.wait_ge(r_dve, 1)
            f(rt(2), rt(0), ACT.Abs).then_inc(r_act, 1)
            f(rt(3), rt(1), ACT.Abs).then_inc(r_act, 1)
            act.wait_ge(r_dve, 4)
            f(rt(2), rt(3), ACT.Exp).then_inc(r_act, 1)
            act.wait_ge(r_dve, 7)
            f(rt(3), rt(0), ACT.Exp, scale=-2.0).then_inc(r_dve, 1)
            act.wait_ge(r_pe, 2)
            for h in range(2):
                ins = nc.scalar.copy(w_t[:, h * T:(h + 1) * T], ps[h][0:E, :])
            ins.then_inc(r_act, 1)

            for cx, cs, co in slots():
                def softplus(i, j, cs=cs):
                    gs = i * 2 + (j + MT * cs)
                    act.wait_ge(pe_dt, gs + 1)
                    act.wait_ge(ld_s[j], (i + PAIRS * cs + 1) * 48)
                    if not (cs == 0 and isinstance(i, int) and i == 0 and j == 0):
                        act.wait_ge(dve_dt, gs)
                    b = ws[:, j, SP_B:SP_B + 1]
                    f(rl[:], p_dt[:], ACT.Relu, bias=b)
                    seq.did(f(lg[:], p_dt[:], ACT.Abs, bias=b))
                    seq.wait()
                    seq.did(f(lg[:], lg[:], ACT.Exp, scale=-1.0))
                    f(aex[:, j, :], ws[:, j, SP_A:SP_A + N], ACT.Exp)
                    seq.wait()
                    f(lg[:], lg[:], ACT.Ln, bias=eps[:, 2:3]).then_inc(act_sp, 1)

                if cs is not None:
                    seq.start(2, 0)
                    softplus(0, 0)
                    seq.end(1)

                def body(i, first, last, turns, cx=cx, cs=cs, co=co):
                    seq.start(0 if cs is None else 2 * (1 if last else 2), i - 1 if turns > 1 else 0)
                    for j in range(2):
                        if cs is not None:
                            gs = i * 2 + (j + MT * cs)
                            for q in range(NU):
                                if q == 0:
                                    act.wait_ge(dve_dt, gs + 1)
                                    act.wait_ge(act_sp, gs + 1)
                                if q == 2 and not (last and j == 1):
                                    softplus(i + (1 if j == 1 else 0), 1 - j)
                                if not (cs == 0 and first and j == 0 and q < 2):
                                    act.wait_ge(dve_h, gs * NU + (q - 1))
                                for n in range(U):
                                    ins = f(da[:, q % 2, n, :], ndt[:], ACT.Exp, scale=aex[:, j, q * U + n:q * U + n + 1])
                                ins.then_inc(act_da, 1)
                        if cx is not None:
                            gx = i * 2 + (j + MT * cx)
                            start = cx == 0 and first and j == 0
                            act.wait_ge(pe_x, gx + 1)
                            if not start:
                                act.wait_ge(dve_conv, gx)
                            nc.scalar.copy(xraw[:, HALO:], p_x[:]).then_inc(act_x, 1)
                            act.wait_ge(dve_conv, gx + 1)
                            if not (cx == 0 and first):
                                act.wait_ge(pe_ss, gx - 1)
                                act.wait_ge(st_u, (gx - 1) * 16)
                            f(uo[:, j, :], xc[:], ACT.Silu).then_inc(act_u, 1)
                            act.wait_ge(pe_g, gx + 1)
                            if not start:
                                act.wait_ge(st_sg, gx * 16)
                            f(sgo[:], p_g[:], ACT.Silu).then_inc(act_sg, 1)
                            if j == 0:
                                gf = i + OT * cx
                                act.wait_ge(pe_f, gf + 1)
                                if not start:
                                    act.wait_ge(st_g, gf * 16)
                                f(fo[:], p_f[:], ACT.Silu, bias=wf[:, FW - 1:FW]).then_inc(act_f, 1)
                    seq.end(turns)

                pairs(act, body)
                if cx is not None:
                    act.wait_ge(pe_ss, MT * (cx + 1))
                    if cs is not None:
                        act.wait_ge(pe_dt, MT * (cs + 1))
                        act.wait_ge(st_bc, 16 * (cs + 1))
                    nc.scalar.copy(ssr[:], p_ss[0:SS, :])
                    f(ssn[:], p_ss[0:SS, :], ACT.Square).then_inc(act_ss, 1)
                    act.wait_ge(pe_ms, cx + 1)
                    f(ssn[:], p_ms[0:SS, :], ACT.Sqrt, bias=eps[0:SS, 1:2]).then_inc(act_rms, 1)

        @block.vector
        def _(dve):
            v = nc.vector
            seq = Seq(dve, dve_seq)
            v.memset(eps[:, 0:1], 1e-5)
            v.memset(eps[:, 1:2], 1e-6)
            v.memset(eps[:, 2:3], 1.0).then_inc(s_eps, 1)
            dve.wait_ge(s_const, 16 * 7)
            def ln_pair(i):
                seq.start(6, i - 1 if not isinstance(i, int) else 0)
                for j in range(2):
                    t = i * 2 + j
                    dve.wait_ge(ln_in[j], (i + 1) * 16)
                    for h in range(2):
                        ins = v.bn_stats(st6[:, j, h, :], lnx[j][:, h * 512:(h + 1) * 512])
                    seq.did(ins)
                    seq.wait()
                    dve.sem_inc(dve_passed, 1)
                    v.bn_aggr(mv[:, j, :], st6[:, j, :, :].rearrange("p a b -> p (a b)")).then_inc(ln_var, 1)
                    dve.wait_ge(ln_std, t + 1)
                    seq.did(v.reciprocal(std[:, 2 + j:3 + j], std[:, j:j + 1]))
                    seq.wait()
                    v.tensor_scalar(lnn[j], lnx[j], mv[:, j, 0:1], std[:, 2 + j:3 + j], ALU.subtract, ALU.mult).then_inc(ln_norm, 1)
                    dve.wait_ge(ln_zh, t + 1)
                    v.tensor_tensor(rt(0)[:, bass.ds(t, 1), :].rearrange("p a b -> p (a b)"), ps[5][0:NA, 0:E], b8t, ALU.add).then_inc(ln_h, 1)
                    seq.did(v.tensor_copy(gmx[:, 7:8], b8t[:, 0:1]))
                seq.end(1 if isinstance(i, int) else TT // 2 - 1)


            ln_pair(0)
            with dve.Fori(1, TT // 2) as i:
                ln_pair(i)
            n_r = [0]

            def did(ins):
                ins.then_inc(r_dve, 1)
                n_r[0] += 1
                dve.wait_ge(r_dve, n_r[0])

            bc = lambda a: a.rearrange("p (a b) -> p a b", b=1).broadcast_to([NA, TT, E])
            dve.wait_ge(r_pe, 1)
            dve.wait_ge(ln_h, TT)
            did(v.tensor_copy(rt(1), ps[6][0:NA, 0:TT * E].rearrange("p (a b) -> p a b", a=TT)))
            dve.wait_ge(r_act, 2)
            v.tensor_reduce(gmx[:, 0:1], rt(2), AX.XY, ALU.max)
            did(v.tensor_reduce(gmx[:, 1:2], rt(3), AX.XY, ALU.max))
            dve.wait_ge(r_pool, 1)
            seq.start(17, 0)
            step = lambda ins: (seq.did(ins), seq.wait())
            step(v.tensor_scalar(gmx[:, 4:6], gmx[:, 2:4], 1e-6, None, ALU.max))
            step(v.reciprocal(gmx[:, 0:2], gmx[:, 4:6]))
            step(v.tensor_scalar(gmx[:, 2:4], gmx[:, 0:2], 0.5, None, ALU.mult))
            step(v.tensor_scalar(rt(0), rt(0), gmx[:, 2:3], None, ALU.mult))
            step(v.tensor_scalar(rt(1), rt(1), gmx[:, 3:4], None, ALU.mult))
            did(v.tensor_tensor(rt(3), rt(1), rt(0), ALU.add))
            step(v.tensor_reduce(r16(0), rt(3), AX.X, ALU.max))
            did(v.tensor_tensor(rt(3), rt(3), bc(r16(0)), ALU.subtract))
            dve.wait_ge(r_act, 3)
            did(v.tensor_reduce(r16(1), rt(2), AX.X, ALU.add))
            step(v.reciprocal(r16(2), r16(1)))
            did(v.tensor_tensor(rt(1), rt(2), bc(r16(2)), ALU.mult))
            for t in range(TT):
                ins = v.max(rt(4)[:, t, :], rt(1)[:, t, :])
            step(ins)
            did(v.tensor_tensor(rt(0), rt(1), rt(4)[:, :, 1:2].broadcast_to([NA, TT, E]), ALU.subtract))
            dve.wait_ge(r_dve, 8)
            step(v.tensor_scalar(rt(3), rt(3), 1.0, None, ALU.add))
            step(v.reciprocal(rt(2), rt(3)))
            step(v.tensor_tensor(rt(0), rt(1), rt(2), ALU.mult))
            step(v.tensor_reduce(r16(3), rt(0), AX.X, ALU.add))
            step(v.tensor_scalar(r16(4), r16(3), 1e-9, None, ALU.add))
            step(v.reciprocal(r16(5), r16(4)))
            step(v.tensor_tensor(rt(5), rt(0), bc(r16(5)), ALU.mult))
            step(v.tensor_copy(gmx[:, 6:7], gmx[:, 4:5]))
            step(v.tensor_copy(gmx[:, 6:7], gmx[:, 4:5]))
            seq.end(1)
            v.tensor_copy(gmx[:, 6:7], gmx[:, 4:5]).then_inc(r_dve, 2)
            dve.wait_ge(r_pe, 3)
            for h in range(2):
                zv = z_t[:, h * L:(h + 1) * L].rearrange("p (a b) -> p a b", b=2)
                pm = ps[2 + h][0:RANK, :].rearrange("p (a b) -> p a b", b=1).broadcast_to([RANK, T, 2])
                ins = v.scalar_tensor_tensor(zv, pm, 0.5, zv, ALU.mult, ALU.mult)
            ins.then_inc(r_zp, 1)

            for cx, cs, co in slots():
                def dt(i, j, cs=cs):
                    gs = i * 2 + (j + MT * cs)
                    dve.wait_ge(act_sp, gs + 1)
                    dve.wait_ge(ld_s[j], (i + PAIRS * cs + 1) * 48)
                    seq.wait()
                    seq.did(v.scalar_tensor_tensor(ndt[:], rl[:], -1.0, lg[:], ALU.mult, ALU.subtract))
                    seq.wait()
                    v.scalar_tensor_tensor(dtu[:], ndt[:], -1.0, ui[:, j, :], ALU.mult, ALU.mult).then_inc(dve_dt, 1)

                if cs is not None:
                    seq.start(1, 0)
                    dt(0, 0)
                    seq.end(1)
                    dve.wait_ge(ld_b, 32 * (cs + 1))

                def body(i, first, last, turns, cx=cx, cs=cs, co=co):
                    carried = cs is not None and cs % HALVES > 0
                    carries = cs is not None and cs % HALVES < HALVES - 1
                    per = 0
                    if cs is not None:
                        per += 2 * (carried + NU + NU * U + 2 * NU - 1 + 1) + 2 - last
                    if cx is not None:
                        per += 2 * (1 + K_CONV)
                    if co is not None:
                        per += 1
                    seq.start(per, i - 1 if turns > 1 else 0)
                    for j in range(2):
                        m = i * 2 + j
                        if cs is not None:
                            gs = i * 2 + (j + MT * cs)

                            def add_up(q):
                                dve.wait_ge(pool_p, gs * NU + (q + 1))
                                p0, p1 = hb[:, q % 2, 0, :], hb[:, q % 2, 1, :]
                                if q == 0:
                                    if not (cs == 0 and first and j == 0):
                                        dve.wait_ge(dve_y, gs)
                                    seq.did(v.tensor_tensor(yacc[:], p0, p1, ALU.add))
                                    return
                                seq.did(v.tensor_tensor(p0, p0, p1, ALU.add))
                                seq.wait()
                                seq.did(v.tensor_tensor(yacc[:], yacc[:], p0, ALU.add))

                            if carried:
                                seq.did(v.tensor_scalar(st[:], states[:, bass.ds(m, 1), :].rearrange("p a b -> p (a b)"), 1.0, None, ALU.mult))
                            for q in range(NU):
                                hq = hb[:, q % 2]
                                if q == 0:
                                    dve.wait_ge(dve_dt, gs + 1)
                                if q > 0:
                                    seq.wait()
                                w = dtu[:].rearrange("p (a t) -> p a t", a=1).broadcast_to([P, U, T])
                                seq.did(v.tensor_tensor(hq, w, bb[:, q * U:(q + 1) * U, :], ALU.mult))
                                seq.wait()
                                dve.wait_ge(act_da, gs * NU + (q + 1))
                                for n in range(U):
                                    init = st[:, q * U + n:q * U + n + 1] if carried else 0.0
                                    seq.did(v.tensor_tensor_scan(hq[:, n, :], da[:, q % 2, n, :], hq[:, n, :], init, ALU.mult, ALU.add))
                                seq.wait()
                                v.tensor_copy(st[:, q * U:(q + 1) * U], hq[:, :, T - 1:T].rearrange("p a b -> p (a b)")).then_inc(dve_h, 1)
                                if q > 0:
                                    add_up(q - 1)
                            if carries:
                                dve.wait_ge(dve_h, gs * NU + NU)
                                v.tensor_scalar(states[:, bass.ds(m, 1), :].rearrange("p a b -> p (a b)"), st[:], 1.0, None, ALU.mult)
                            if not (last and j == 1):
                                dt(i + (1 if j == 1 else 0), 1 - j)
                        if cx is not None:
                            gx = i * 2 + (j + MT * cx)
                            dve.wait_ge(act_x, gx + 1)
                            if not (cx == 0 and first and j == 0):
                                dve.wait_ge(act_u, gx)
                            dve.wait_ge(ld_x[j], (i + PAIRS * cx + 1) * 16)
                            if not (cx == 0 and first and j == 0):
                                dve.wait_ge(dve_conv, gx)
                            if cx % HALVES == 0:
                                seq.did(v.memset(xraw[:, 0:HALO], 0.0))
                            else:
                                seq.did(v.tensor_scalar(xraw[:, 0:HALO], tails[:, bass.ds(m, 1), :].rearrange("p a b -> p (a b)"), 1.0, None, ALU.mult))
                            seq.wait()
                            tap = lambda k: wx[:, j, WXX + k:WXX + k + 1]
                            seq.did(v.tensor_scalar(xc[:], xraw[:, 0:T], tap(0), tap(K_CONV), ALU.mult, ALU.add))
                            for k in range(1, K_CONV):
                                seq.wait()
                                seq.did(v.scalar_tensor_tensor(xc[:], xraw[:, k:k + T], tap(k), xc[:], ALU.mult, ALU.add))
                            seq.wait()
                            v.tensor_scalar(tails[:, bass.ds(m, 1), :].rearrange("p a b -> p (a b)"), xraw[:, T:T + HALO], 1.0, None, ALU.mult).then_inc(dve_conv, 1)
                        if cs is not None:
                            add_up(NU - 1)
                            seq.wait()
                            seq.did(v.scalar_tensor_tensor(yacc[:], ui[:, j, :], ws[:, j, SP_D:SP_D + 1], yacc[:], ALU.mult, ALU.add))
                            seq.wait()
                            if not (cs == 0 and first and j == 0):
                                dve.wait_ge(st_y, gs * 16)
                            v.tensor_tensor(yo[:], yacc[:], sgi[:, j, :], ALU.mult).then_inc(dve_y, 1)
                        if co is not None and j == 1:
                            go_n = i + OT * co
                            dve.wait_ge(pe_o, go_n + 1)
                            dve.wait_ge(ld_o, (go_n + 1) * 48)
                            seq.did(v.tensor_tensor(go[:], p_o[:], go[:], ALU.mult))
                            seq.wait()
                            v.tensor_tensor(xo[:], xo[:], go[:], ALU.add).then_inc(dve_o, 1)
                    seq.end(turns)

                pairs(dve, body)
                if cx is not None:
                    dve.wait_ge(act_rms, cx + 1)
                    seq.start(1, 0)
                    seq.did(v.reciprocal(ssn[:], ssn[:]))
                    seq.wait()
                    v.tensor_tensor(ssn[:], ssn[:], ssr[:], ALU.mult).then_inc(dve_ssn, 1)
                    seq.end(1)

        @block.gpsimd
        def _(pool):
            pool.wait_ge(r_dve, 2)
            nc.gpsimd.partition_all_reduce(gmx[:, 2:4], gmx[:, 0:2], NA, bass.bass_isa.ReduceOp.max).then_inc(r_pool, 1)
            for cx, cs, co in slots():
                if cs is None:
                    continue
                pool.wait_ge(ld_c, 32 * (cs + 1))

                def body(i, first, last, turns, cs=cs):
                    for j in range(2):
                        gs = i * 2 + (j + MT * cs)
                        for q in range(NU):
                            pool.wait_ge(dve_h, gs * NU + (q + 1))
                            nc.gpsimd.tensor_tensor(hb[:, q % 2], hb[:, q % 2], cb[:, q * U:(q + 1) * U, :], ALU.mult).then_inc(pool_p, 1)

                pairs(pool, body)


_OUTS = ("out", (NC, OT, P, T))


def kernel(L0_attn_hidden_states, L0_attn_W_in, L0_attn_conv_w, L0_attn_conv_b, L0_attn_W_x, L0_attn_W_dt,
           L0_attn_b_dt, L0_attn_A_log, L0_attn_D, L0_attn_W_out, L0_ffn_W, L0_ffn_b, L0_ffn_A, L0_ffn_Bmat,
           L0_ffn_LiMEs):
    import numpy as np
    import concourse.bacc as bacc
    from concourse.bass_utils import run_bass_kernel_spmd

    def tiles(w, k):
        return w.reshape(-1, P, k, P).transpose(0, 3, 2, 1).reshape(-1, P, k * P)

    def cols(v):
        return v.reshape(-1, P, v.size // v.shape[0])

    x = L0_attn_hidden_states.reshape(TOK, H)
    f32 = x.dtype
    w_in = tiles(L0_attn_W_in, KH)
    w_dt = np.zeros((MT, P, P), f32)
    w_dt[:, :R] = L0_attn_W_dt.reshape(MT, P, R).transpose(0, 2, 1)
    b_mat = np.zeros((OT, P, P), f32)
    b_mat[:, :RANK] = L0_ffn_Bmat.reshape(RANK, OT, P).transpose(1, 0, 2)
    blk = np.zeros((SS, SS), f32)
    for a, n in ((0, R), (R, N), (R + N, N)):
        blk[a:a + n, a:a + n] = 1.0 / n
    arrays = {
        "x": np.concatenate([x.reshape(TT, P, H), x.reshape(TT, P, H)[:2]]),
        "xt": x.reshape(NC, T, OT, P).transpose(0, 2, 3, 1),
        "w_in": np.concatenate([w_in[:MT], L0_attn_W_x.T.reshape(MT, P, SS), cols(L0_attn_conv_w),
                                cols(L0_attn_conv_b)], axis=2),
        "w_s": np.concatenate([cols(L0_attn_A_log), cols(L0_attn_b_dt), cols(L0_attn_D), w_dt], axis=2),
        "w_g": w_in[MT:],
        "w_o": tiles(L0_attn_W_out, MT),
        "w_f": np.concatenate([tiles(L0_ffn_W, KH), b_mat, cols(L0_ffn_b)], axis=2),
        "w8": L0_ffn_W[:E].reshape(E, KH, P).transpose(2, 1, 0),
        "a_r": L0_ffn_A.reshape(KH, P, RANK).transpose(1, 0, 2),
        "lime": L0_ffn_LiMEs,
        "lime_t": L0_ffn_LiMEs.T,
        "b8": np.broadcast_to(L0_ffn_b[:E], (NA, E)),
        "ident": np.eye(P, dtype=f32),
        "blk": blk,
    }
    nc = bacc.Bacc("TRN2", target_bir_lowering=False, num_devices=1)
    arrays = {k: np.ascontiguousarray(v) for k, v in arrays.items()}
    args = [nc.dram_tensor(k, v.shape, F32, kind="ExternalInput").ap() for k, v in arrays.items()]
    out = nc.dram_tensor(_OUTS[0], _OUTS[1], F32, kind="ExternalOutput").ap()
    build(nc, *args, out)
    r = run_bass_kernel_spmd(nc, [arrays], core_ids=[0]).results[0]["out"]
    return r.transpose(0, 3, 1, 2).reshape(BATCH, L, H)
```

```python
from contextlib import ExitStack

import concourse.bass as bass
from concourse import mybir

F32 = mybir.dt.float32
ALU = mybir.AluOpType
ACT = mybir.ActivationFunctionType
AX = mybir.AxisListType

P = 128
BATCH, L, H = 2, 1024, 1024
D_IN, N, K_CONV, R = 2048, 16, 4, 64
E, RANK = 8, 32
TOK = BATCH * L
T = 512
NC = TOK // T
HALVES = L // T
KH = H // P
MT = D_IN // P
OT = H // P
SS = R + 2 * N
TT = TOK // P
NA = P // 2
U = 2
NU = N // U
RING = 4
PE_UNITS = ((1, 5), (0, 1, 3, 5), (0, 1, 3, 5), (0, 1, 2, 3, 4, 5, 6))
PB = 4
PAIRS = MT // 2
WX = KH * P
WXW = SS + K_CONV + 1
SP_A, SP_B, SP_D, SP_W = 0, N, N + 1, N + 2
SPW = SP_W + P
FW = KH * P + P + 1
HALO = K_CONV - 1


class Seq:

    def __init__(self, eng, sem):
        self.eng, self.sem, self.base, self.turn, self.n = eng, sem, 0, 0, 0

    def start(self, per, turn):
        self.per, self.turn, self.n = per, turn, 0

    def end(self, turns):
        assert self.n == self.per, (self.n, self.per)
        self.base += self.per * turns

    def did(self, ins):
        ins.then_inc(self.sem, 1)
        self.n += 1
        return self.n

    def wait(self, n=None):
        n = self.n if n is None else n
        self.eng.wait_ge(self.sem, self.turn * self.per + (self.base + n))


def build(nc, x, xt, w_in, w_x, w_s, w_g, w_o, w_f, w8, a_r, lime, lime_t, b8, ident, blk, out):
    ctx = ExitStack()
    with ctx:
        sb = lambda name, shape: ctx.enter_context(nc.sbuf_tensor(name, shape, F32))
        sem = lambda name: ctx.enter_context(nc.semaphore(name))
        dram = lambda name, shape: nc.dram_tensor(name, shape, F32, kind="Internal").ap()

        xn_d = dram("xn_d", (TT, P, KH, P))
        zp_d = dram("zp_d", (NC, RANK, T))
        u_d = dram("u_d", (NC, MT, P, T))
        sg_d = dram("sg_d", (NC, MT, P, T))
        g_d = dram("g_d", (NC, OT, P, T))
        y_d = dram("y_d", (NC, MT, P, T))
        bc_d = dram("bc_d", (NC, 2, N * T))

        idt = sb("idt", [P, P])
        blkt = sb("blkt", [SS, SS])
        eps = sb("eps", [P, 3])
        bb = sb("bb", [P, N, T])
        cb = sb("cb", [P, N, T])
        hb = sb("hb", [P, RING, U, T])
        da = sb("da", [P, 2, U, T])
        yb = sb("yb", [P, MT, T])
        xn1 = sb("xn1", [P, KH, T])
        xn0 = yb[:, 0:KH, :]
        wx = sb("wx", [P, 2, WX])
        wxx = sb("wxx", [P, 2, WXW])
        wg = sb("wg", [P, 2, WX])
        wf = sb("wf", [P, FW])
        wo = sb("wo", [P, MT * P])
        ws = sb("ws", [P, 2, SPW])
        xraw = sb("xraw", [P, T + HALO])
        tails = sb("tails", [P, MT, HALO])
        xc = sb("xc", [P, T])
        uo = sb("uo", [P, 2, T])
        sgo = sb("sgo", [P, T])
        fo = sb("fo", [P, T])
        ui = sb("ui", [P, 2, T])
        sgi = sb("sgi", [P, 2, T])
        rl = sb("rl", [P, T])
        lg = sb("lg", [P, T])
        ndt = sb("ndt", [P, T])
        dtu = sb("dtu", [P, T])
        aex = sb("aex", [P, 2, N])
        st = sb("st", [P, N])
        states = sb("states", [P, MT, N])
        yacc = sb("yacc", [P, T])
        xo = sb("xo", [P, T])
        go = sb("go", [P, T])
        ssn_zp = sb("ssn_zp", [P, 2, T])
        ssn, zp = ([ssn_zp[a:b, h, :] for h in range(2)] for a, b in ((0, SS), (SS, P)))
        ssr = xc[0:SS, :]
        ps = [ctx.enter_context(nc.psum_tensor(f"ps{k}", [P, T], F32)) for k in range(8)]
        p_x, (p_g, p_dt, p_ss, p_o, p_f, p_y) = (ps[0], ps[6]), (*ps[1:6], ps[7])
        p_ms = p_ss

        flat = lambda t: t[:].rearrange("p a b -> p (a b)")
        lnx = [bb[:, 2 * j:2 * j + 2, :].rearrange("p a b -> p (a b)") for j in range(2)]
        lnn = [bb[:, 4 + 2 * j:6 + 2 * j, :].rearrange("p a b -> p (a b)") for j in range(2)]
        lnt = [bb[:, 8 + 2 * j:10 + 2 * j, :].rearrange("p a b -> p (a b)").rearrange("p (k t) -> p k t", k=KH) for j in range(2)]
        z_t = cb[0:RANK, 0:TOK // T, :].rearrange("p a b -> p (a b)")
        w8t = cb[:, 4, 0:KH * E].rearrange("p (k e) -> p k e", k=KH)
        art = cb[:, 5, 0:KH * RANK].rearrange("p (k e) -> p k e", k=KH)
        limet = cb[0:E, 6, 0:RANK]
        limett = cb[0:RANK, 6, RANK:RANK + E]
        b8t = cb[0:NA, 7, 0:E]
        w_t = cb[0:E, 8:10, :].rearrange("p a b -> p (a b)")
        rt = lambda k: cb[0:NA, 10 + k // 4, (k % 4) * TT * E:(k % 4 + 1) * TT * E].rearrange("p (a b) -> p a b", a=TT)
        small = cb[:, 14, :]
        st6 = small[:, 0:24].rearrange("p (j a b) -> p j a b", j=2, a=2)
        mv = small[:, 24:28].rearrange("p (j a) -> p j a", j=2)
        std = small[:, 28:32]
        gmx = small[0:NA, 40:48]
        r16 = lambda k: small[0:NA, 64 + 16 * k:80 + 16 * k]

        s_const, s_eps = sem("s_const"), sem("s_eps")
        ln_in = [sem("ln_in0"), sem("ln_in1")]
        ln_var, ln_std, ln_norm = sem("ln_var"), sem("ln_std"), sem("ln_norm")
        ln_tr, ln_tc, ln_zh = sem("ln_tr"), sem("ln_tc"), sem("ln_zh")
        ln_z, ln_h, ln_st = sem("ln_z"), sem("ln_h"), sem("ln_st")
        r_pe, r_act, r_dve, r_pool, r_zp = sem("r_pe"), sem("r_act"), sem("r_dve"), sem("r_pool"), sem("r_zp")
        ld_x = [sem("ld_x0"), sem("ld_x1")]
        ld_w = [sem("ld_w0"), sem("ld_w1")]
        ld_g = [sem("ld_g0"), sem("ld_g1")]
        ld_s = [sem("ld_s0"), sem("ld_s1")]
        ld_o = [sem("ld_o0"), sem("ld_o1")]
        ld_f, ld_r, ld_xn = (sem(n) for n in ("ld_f", "ld_r", "ld_xn"))
        ld_y = [sem("ld_y0"), sem("ld_y1")]
        ld_b = [sem(f"ld_b{n}") for n in range(PB)]
        ld_c = [sem(f"ld_c{n}") for n in range(PB)]
        st_u = [sem("st_u0"), sem("st_u1")]
        st_sg, st_g, st_y, st_o, st_bc = (sem(n) for n in ("st_sg", "st_g", "st_y", "st_o", "st_bc"))
        pe_x, act_x, dve_conv, act_u, pe_ss = (sem(n) for n in ("pe_x", "act_x", "dve_conv", "act_u", "pe_ss"))
        pe_g, act_sg, pe_f, act_f = (sem(n) for n in ("pe_g", "act_sg", "pe_f", "act_f"))
        act_ss, pe_ms, act_rms, dve_ssn = (sem(n) for n in ("act_ss", "pe_ms", "act_rms", "dve_ssn"))
        pe_g0, act_sg0, st_sg0, pe_f0, act_f0, st_g0 = (
            sem(n) for n in ("pe_g0", "act_sg0", "st_sg0", "pe_f0", "act_f0", "st_g0"))
        pe_dt, act_sp, dve_dt, act_da, dve_h, pool_p, dve_y = (
            sem(n) for n in ("pe_dt", "act_sp", "dve_dt", "act_da", "dve_h", "pool_p", "dve_y"))
        pe_y = sem("pe_y")
        pe_o, dve_o = sem("pe_o"), sem("dve_o")
        sp_passed, dve_passed = sem("sp_passed"), sem("dve_passed")
        act_seq, dve_seq = sem("act_seq"), sem("dve_seq")

        block = ctx.enter_context(nc.Block())

        chunk = lambda c: c if 0 <= c < NC else None

        class Pair:

            def __init__(self, i, s):
                self.i, self.turns, self.turn = i, 1, 0
                self.cx = chunk(s)
                self.k, d = (PAIRS - 1, 1) if isinstance(i, int) and i == 0 else (i - 1, 0)
                self.cs, self.co = chunk(s - 1 - d), chunk(s - 2 - d)
                if not isinstance(i, int):
                    self.turns, self.turn = PAIRS - 3, i - 2
                self.first, self.last = (isinstance(i, int) and i == n for n in (0, PAIRS - 1))
                self.s_first, self.s_last = (isinstance(self.k, int) and self.k == n for n in (0, PAIRS - 1))
                self.gates = self.cx is not None and self.cx > 0
                self.gates0 = self.cx == 1

            def x(self, j):
                return self.i * 2 + (j + MT * self.cx)

            def s(self, j):
                return self.k * 2 + (j + MT * self.cs)

            def next_s(self, j):
                if self.s_last and j == 1:
                    return (self.cs + 1, 0, 0) if self.cs + 1 < NC else None
                return self.cs, self.k + j, 1 - j

            def start(self, j=0):
                return self.cx == 0 and self.first and j == 0

            def s_start(self, j=0):
                return self.cs == 0 and self.s_first and j == 0

        def run(eng, body, before_s=None, after_x=None, before_x=None):
            for s in range(NC + 3):
                if before_x:
                    before_x(chunk(s), chunk(s - 2))
                body(Pair(0, s))
                if s == NC + 2:
                    break
                if before_s:
                    before_s(chunk(s - 1), chunk(s - 2))
                body(Pair(1, s))
                with eng.Fori(2, PAIRS - 1) as i:
                    body(Pair(i, s))
                body(Pair(PAIRS - 1, s))
                if after_x and chunk(s) is not None:
                    after_x(s)

        @block.sync
        def _(sp):
            def wait(s, count):
                sp.wait_ge(s, count)
                if not isinstance(count, int):
                    sp.sem_inc(sp_passed, 1)

            for dst, src in ((idt[:], ident), (blkt[:], blk), (w8t, w8), (art, a_r), (limet, lime),
                             (limett, lime_t), (b8t, b8)):
                sp.dma_start(dst, src).then_inc(s_const, 16)

            def ln_load(t, j, pair):
                sp.dma_start(lnx[j], x[t]).then_inc(ln_in[j], 16)

            ln_load(0, 0, 0)
            ln_load(1, 1, 0)
            def ln_pair(i):
                for j in range(2):
                    t = i * 2 + j
                    wait(ln_norm, t + 1)
                    wait(ln_tc, t + 1)
                    sp.dma_start(xn_d[t], lnt[j]).then_inc(ln_st, 16)
                    nxt = t + 2
                    sp.dma_start(lnx[j], x[nxt]).then_inc(ln_in[j], 16)

            ln_pair(0)
            with sp.Fori(1, TT // 2) as i:
                ln_pair(i)
            wait(ln_in[0], 16 * (TT // 2 + 1))
            wait(ln_in[1], 16 * (TT // 2 + 1))
            wait(ln_st, 16 * TT)
            wait(r_zp, 1)
            for c in range(NC):
                sp.dma_start(zp_d[c], z_t[:, c * T:(c + 1) * T]).then_inc(ln_st, 16)
            wait(ln_st, 16 * (TT + NC))

            def load_x(m, j):
                sp.dma_start(wx[:, j, :], w_in[m]).then_inc(ld_x[j], 16)

            def load_w(m, j, gates):
                sp.dma_start(wxx[:, j, :], w_x[m]).then_inc(ld_w[j], 16)
                if gates:
                    sp.dma_start(wg[:, j, :], w_g[m]).then_inc(ld_g[j], 16)

            def load_s(c, m, j):
                sp.dma_start(ws[:, j, :], w_s[m]).then_inc(ld_s[j], 16)
                sp.dma_start(ui[:, j, :], u_d[c, m]).then_inc(ld_s[j], 16)
                sp.dma_start(sgi[:, j, :], sg_d[c, m]).then_inc(ld_s[j], 16)

            def load_o(o, h):
                w = MT * P // 2
                sp.dma_start(wo[:, h * w:(h + 1) * w], w_o[o, :, h * w:(h + 1) * w]).then_inc(ld_o[h], 16)

            def load_bc(c, n):
                a, b = n * N * T // PB, (n + 1) * N * T // PB
                sp.dma_start(flat(bb)[:, a:b], bc_d[c, 0:1, a:b].partition_broadcast(P)).then_inc(ld_b[n], 16)
                if c > 0:
                    wait(pool_p, NU * (MT * c - 1) + NU // PB * (n + 1))
                sp.dma_start(flat(cb)[:, a:b], bc_d[c, 1:2, a:b].partition_broadcast(P)).then_inc(ld_c[n], 16)

            def load_xn(cx):
                xn = xn1 if cx > 0 else xn0
                for r in range(T // P):
                    sp.dma_start(xn[:, :, r * P:(r + 1) * P], xn_d[cx * (T // P) + r]).then_inc(ld_xn, 16)
                sp.dma_start(zp[cx % 2], zp_d[cx]).then_inc(ld_xn, 16)

            def load_y(co, h):
                m = MT // 2 * h
                wait(st_y, 16 * (MT * co + MT // 2 * (h + 1)))
                sp.dma_start(yb[:, m:m + MT // 2, :], y_d[co, m:m + MT // 2].rearrange("m p t -> p m t")).then_inc(ld_y[h], 16)

            def before_x(cx, co):
                if cx == 0:
                    load_x(0, 0)
                    load_w(0, 0, False)
                    load_xn(0)
                    load_x(1, 1)
                if co == 0:
                    wait(pe_g0, MT)
                    wait(pe_f0, OT)
                    load_o(0, 0)
                    load_y(0, 0)

            def before_s(cs, co):
                if cs == 0:
                    wait(st_sg0, 16 * 1)
                    load_s(0, 0, 0)
                    for n in range(PB):
                        load_bc(0, n)
                if cs is None:
                    load_xn(1)
                if co is not None:
                    wait(st_g if co else st_g0, 16 * OT * max(co, 1))
                    if co > 0:
                        wait(pe_o, 2 * OT * co)
                    load_o(0, 1)
                    load_y(co, 1)

            def after_x(cx):
                if cx + 1 < NC:
                    if cx > 0:
                        wait(pe_x, MT * (cx + 1))
                        wait(pe_g, MT * cx)
                        wait(pe_f, OT * cx)
                        load_xn(cx + 1)
                        wait(act_f, OT * cx)
                    load_x(0, 0)
                    wait(pe_ss, MT * (cx + 1) - 1)
                    wait(dve_conv, MT * (cx + 1) - 1)
                    load_w(0, 0, True)
                    wait(pe_x, MT * (cx + 1))
                    load_x(1, 1)
                    sp.dma_start(wf[:], w_f[0]).then_inc(ld_f, 16)
                wait(dve_ssn, cx + 1)
                sp.dma_start(bc_d[cx].rearrange("a (n t) -> (a n) t", n=N), ssn_zp[R:SS, cx % 2, :]).then_inc(st_bc, 16)
                wait(st_bc, 16 * (cx + 1))
                for j in range(2):
                    wait(st_u[j], 16 * PAIRS * (cx + 1))
                if cx > 0:
                    wait(st_sg, 16 * MT * cx)

            def body(p):
                for j in range(2):
                    if p.cs is not None:
                        nxt = p.next_s(j)
                        if nxt:
                            c, k, nj = nxt
                            if not p.s_start(j):
                                wait(st_y, p.s(j) * 16)
                            if c == 0:
                                wait(st_sg0, (k * 2 + (nj + 1)) * 16)
                            load_s(c, k * 2 + nj, nj)
                    if p.cx is not None:
                        gx = p.x(j)
                        if not p.last:
                            wait(pe_x, gx + 1)
                            load_x(p.i * 2 + (j + 2), j)
                        if not (p.last and j == 1):
                            if not p.start(j):
                                wait(pe_ss, gx)
                                wait(dve_conv, gx)
                                if p.cx > 1 or p.cx == 1 and not (p.first and j == 0):
                                    wait(pe_g, gx - MT)
                            load_w(p.i * 2 + (j + 1), 1 - j, p.gates)
                    if p.cs is not None and p.s_last and j == 1 and nxt:
                        for n in range(PB):
                            wait(dve_h, NU * (MT * nxt[0] - 1) + NU // PB * (n + 1))
                            load_bc(nxt[0], n)
                    if p.cx is not None:
                        if p.gates0:
                            wait(act_sg0, gx - (MT - 1))
                            sp.dma_start(sg_d[0, p.i * 2 + j], go[:]).then_inc(st_sg0, 16)
                            if j == 0:
                                wait(act_f0, p.i + 1)
                                sp.dma_start(g_d[0, p.i], xo[:]).then_inc(st_g0, 16)
                        wait(act_u, gx + 1)
                        sp.dma_start(u_d[p.cx, p.i * 2 + j], uo[:, j, :]).then_inc(st_u[j], 16)
                        if p.gates:
                            wait(act_sg, gx - (MT - 1))
                            sp.dma_start(sg_d[p.cx, p.i * 2 + j], sgo[:]).then_inc(st_sg, 16)
                            if j == 1:
                                wait(act_f, p.i + (OT * (p.cx - 1) + 1))
                                sp.dma_start(g_d[p.cx, p.i], fo[:]).then_inc(st_g, 16)
                                if not p.last:
                                    sp.dma_start(wf[:], w_f[p.i + 1]).then_inc(ld_f, 16)
                    if p.co is not None:
                        n_o = p.k + OT * p.co
                        if j == 0:
                            if p.co > 0 or not p.s_first:
                                wait(st_o, n_o * 16)
                            sp.dma_start(xo[:], xt[p.co, p.k]).then_inc(ld_r, 16)
                            sp.dma_start(go[:], g_d[p.co, p.k]).then_inc(ld_r, 16)
                        if not p.s_last:
                            wait(pe_o, n_o * 2 + (j + 1))
                            load_o(p.k + 1, j)
                        elif j == 0 and p.co + 1 < NC:
                            wait(pe_o, n_o * 2 + 1)
                            load_o(0, 0)
                            load_y(p.co + 1, 0)
                        if j == 1:
                            wait(dve_o, n_o + 1)
                            sp.dma_start(out[p.co, p.k], xo[:]).then_inc(st_o, 16)
                    if p.cs is not None:
                        wait(dve_y, p.s(j) + 1)
                        sp.dma_start(y_d[p.cs, p.k * 2 + j], sgi[:, j, :]).then_inc(st_y, 16)

            run(sp, body, before_s, after_x, before_x)
            sp.wait_ge(st_o, 16 * OT * NC)

        @block.tensor
        def _(pe):
            mm = nc.tensor.matmul

            pe.wait_ge(s_const, 16 * 7)
            def ln_z_h(t, j):
                pe.wait_ge(ln_tc, t + 1)
                if not (isinstance(t, int) and t == 0):
                    pe.wait_ge(ln_z, t)
                    pe.wait_ge(ln_h, t)
                for k in range(KH):
                    mm(ps[4][0:RANK, 0:P], art[:, k, :], lnt[j][:, k, :], start=(k == 0), stop=(k == KH - 1))
                for k in range(KH):
                    ins = mm(ps[5][0:NA, 0:E], lnt[j][:, k, 1:P:2], w8t[:, k, :], start=(k == 0), stop=(k == KH - 1))
                ins.then_inc(ln_zh, 1)

            def ln_pair(i):
                for j in range(2):
                    t = i * 2 + j
                    pe.wait_ge(ln_norm, t + 1)
                    if not isinstance(i, int):
                        pe.wait_ge(ln_tc, t - 1)
                    for k in range(KH):
                        ins = nc.tensor.transpose(ps[2 * j + k // 4][:, (k % 4) * P:(k % 4 + 1) * P],
                                                  lnn[j][:, k * P:(k + 1) * P], idt[:])
                    ins.then_inc(ln_tr, 1)
                    if not (isinstance(i, int) and j == 0):
                        ln_z_h(t - 1, 1 - j)

            ln_pair(0)
            with pe.Fori(1, TT // 2) as i:
                ln_pair(i)
            ln_z_h(TT - 1, 1)
            pe.wait_ge(ln_z, TT)
            for t in range(TT):
                ins = mm(ps[6][0:NA, t * E:(t + 1) * E], z_t[:, t * P + 1:(t + 1) * P:2], limett, start=True, stop=True)
            ins.then_inc(r_pe, 1)
            pe.wait_ge(r_dve, 10)
            for t in range(TT):
                ins = nc.tensor.transpose(ps[t // 8][0:E, (t % 8) * NA:(t % 8 + 1) * NA], rt(5)[:, t, :], idt[0:NA, 0:NA])
            ins.then_inc(r_pe, 1)
            pe.wait_ge(r_act, 4)
            for h in range(2):
                ins = mm(ps[2 + h][0:RANK, :], limet, w_t[:, h * T:(h + 1) * T], start=True, stop=True)
            ins.then_inc(r_pe, 1)

            pe.wait_ge(r_zp, 1)

            def before_x(cx, co):
                if cx is not None:
                    pe.wait_ge(ld_xn, 16 * (T // P + 1) * (cx + 1))

            def dt_product(c, k, j):
                pe.wait_ge(ld_s[j], (k + (PAIRS * c + 1)) * 48)
                if isinstance(k, int) and k == 0 and j == 0:
                    pe.wait_ge(dve_ssn, c + 1)
                if not (c == 0 and isinstance(k, int) and k == 0 and j == 0):
                    pe.wait_ge(act_sp, k * 2 + (j + MT * c))
                mm(p_dt[:], ws[0:R, j, SP_W:SPW], ssn[c % 2][0:R, :], start=True, stop=True).then_inc(pe_dt, 1)

            def before_s(cs, co):
                if cs == 0:
                    dt_product(0, 0, 0)

            def add_up(p, j, qs):
                units = PE_UNITS[p.cs]
                for q in qs:
                    if q not in units:
                        continue
                    pe.wait_ge(pool_p, p.s(j) * NU + (q + 1))
                    if q == units[0] and not p.s_start(j):
                        pe.wait_ge(dve_y, p.s(j))
                    for n in range(U):
                        ins = mm(p_y[:], idt[:], hb[:, q % RING, n, :], start=(q == units[0] and n == 0),
                                 stop=(q == units[-1] and n == U - 1))
                    ins.then_inc(pe_y, 1)

            def project(bank, w, src):
                for k in range(KH):
                    ins = mm(bank[:], w[:, k * P:(k + 1) * P], src[:, k, :], start=(k == 0), stop=(k == KH - 1))
                return ins

            def feed_forward(src, z):
                for k in range(KH):
                    mm(p_f[:], wf[:, k * P:(k + 1) * P], src[:, k, :], start=(k == 0), stop=False)
                return mm(p_f[:], wf[SS:P, KH * P:KH * P + P], z, start=False, stop=True)

            def half(p, h):
                n_o = p.k + OT * p.co
                pe.wait_ge(ld_o[h], (n_o + 1) * 16)
                if p.s_first:
                    pe.wait_ge(ld_y[h], 16 * (p.co + 1))
                if h == 0 and p.co == 0 and p.s_first:
                    pe.wait_ge(act_sg0, MT)
                elif h == 0:
                    pe.wait_ge(dve_o, n_o)
                for k in range(MT // 2 * h, MT // 2 * (h + 1)):
                    ins = mm(p_o[:], wo[:, k * P:(k + 1) * P], yb[:, k, :], start=(k == 0), stop=(k == MT - 1))
                ins.then_inc(pe_o, 1)

            def body(p):
                for j in range(2):
                    if p.cx is not None:
                        gx = p.x(j)
                        xn = xn1 if p.cx > 0 else xn0
                        pe.wait_ge(ld_x[j], (p.i + (PAIRS * p.cx + 1)) * 16)
                        if not (p.cx == 0 and p.first):
                            pe.wait_ge(act_x, gx - 1)
                        project(p_x[j], wx[:, j, :], xn).then_inc(pe_x, 1)
                    if p.cs is not None:
                        add_up(p, j, (0, 1))
                        if p.next_s(j):
                            dt_product(*p.next_s(j))
                    if p.cx is not None:
                        if not (p.first and j == 0):
                            pe.wait_ge(act_u, gx)
                            if p.first and j == 1 and p.cx > 0:
                                pe.wait_ge(act_ss, p.cx)
                            pe.wait_ge(ld_w[1 - j], (p.i + (PAIRS * p.cx + j)) * 16)
                            mm(p_ss[0:SS, :], wxx[:, 1 - j, 0:SS], uo[:, 1 - j, :],
                               start=(p.first and j == 1), stop=False).then_inc(pe_ss, 1)
                    if p.gates0:
                        pe.wait_ge(ld_g[j], (p.i + 1) * 16)
                        if not (p.first and j == 0):
                            pe.wait_ge(act_sg0, gx - MT)
                        project(p_o, wg[:, j, :], xn0).then_inc(pe_g0, 1)
                        if j == 0:
                            pe.wait_ge(ld_f, (p.i + 1) * 16)
                            if not p.first:
                                pe.wait_ge(act_f, p.i)
                            feed_forward(xn0, zp[0]).then_inc(pe_f0, 1)
                    if p.cs is not None:
                        add_up(p, j, (2, 3))
                    if p.gates:
                        pe.wait_ge(ld_g[j], (p.i + (PAIRS * (p.cx - 1) + 1)) * 16)
                        if not (p.cx == 1 and p.first and j == 0):
                            pe.wait_ge(act_sg, gx - MT)
                        project(p_g, wg[:, j, :], xn).then_inc(pe_g, 1)
                    if p.cs is not None:
                        add_up(p, j, (4,))
                    if p.co is not None and j == 0:
                        half(p, 0)
                    if p.gates and j == 1:
                        gf = p.i + OT * (p.cx - 1)
                        pe.wait_ge(ld_f, (gf + 1) * 16)
                        if p.gates0:
                            pe.wait_ge(act_f0, p.i + 1)
                        else:
                            pe.wait_ge(act_f, gf)
                        feed_forward(xn, zp[p.cx % 2]).then_inc(pe_f, 1)
                    if p.cs is not None:
                        add_up(p, j, (5, 6))
                    if p.co is not None and j == 0:
                        half(p, 1)

            def after_x(cx):
                pe.wait_ge(act_u, MT * (cx + 1))
                pe.wait_ge(ld_w[1], PAIRS * (cx + 1) * 16)
                mm(p_ss[0:SS, :], wxx[:, 1, 0:SS], uo[:, 1, :], start=False, stop=True).then_inc(pe_ss, 1)
                pe.wait_ge(act_ss, cx + 1)
                mm(p_ms[0:SS, :], blkt[:], ssn[cx % 2], start=True, stop=True).then_inc(pe_ms, 1)

            run(pe, body, before_s, after_x, before_x)

        @block.scalar
        def _(act):
            seq = Seq(act, act_seq)
            f = nc.scalar.activation
            act.wait_ge(s_eps, 1)
            def ln_copy_z(t):
                act.wait_ge(ln_zh, t + 1)
                nc.scalar.copy(z_t[:, bass.ds(t * P, P)], ps[4][0:RANK, 0:P]).then_inc(ln_z, 1)

            def ln_pair(i):
                for j in range(2):
                    t = i * 2 + j
                    act.wait_ge(ln_var, t + 1)
                    f(std[:, j:j + 1], mv[:, j, 1:2], ACT.Sqrt, bias=eps[:, 0:1]).then_inc(ln_std, 1)
                    act.wait_ge(ln_tr, t + 1)
                    if not isinstance(i, int):
                        act.wait_ge(ln_st, (t - 1) * 16)
                        act.wait_ge(ln_zh, t - 1)
                    for h in range(2):
                        ins = nc.scalar.copy(lnt[j][:, 4 * h:4 * h + 4, :], ps[2 * j + h][:].rearrange("p (a b) -> p a b", a=4))
                    ins.then_inc(ln_tc, 1)
                    if not (isinstance(i, int) and j == 0):
                        ln_copy_z(t - 1)

            ln_pair(0)
            with act.Fori(1, TT // 2) as i:
                ln_pair(i)
            ln_copy_z(TT - 1)
            act.wait_ge(r_dve, 1)
            f(rt(2), rt(0), ACT.Abs).then_inc(r_act, 1)
            f(rt(3), rt(1), ACT.Abs).then_inc(r_act, 1)
            act.wait_ge(r_dve, 4)
            f(rt(2), rt(3), ACT.Exp).then_inc(r_act, 1)
            act.wait_ge(r_dve, 7)
            f(rt(3), rt(0), ACT.Exp, scale=-2.0).then_inc(r_dve, 1)
            act.wait_ge(r_pe, 2)
            for h in range(2):
                ins = nc.scalar.copy(w_t[:, h * T:(h + 1) * T], ps[h][0:E, :])
            ins.then_inc(r_act, 1)

            def softplus(c, k, j, part):
                b = ws[:, j, SP_B:SP_B + 1]
                if part == 0:
                    act.wait_ge(pe_dt, k * 2 + (j + MT * c + 1))
                    act.wait_ge(ld_s[j], (k + (PAIRS * c + 1)) * 48)
                    if not (c == 0 and isinstance(k, int) and k == 0 and j == 0):
                        act.wait_ge(dve_dt, k * 2 + (j + MT * c))
                    seq.did(f(lg[:], p_dt[:], ACT.Abs, bias=b))
                if part == 1:
                    f(rl[:], p_dt[:], ACT.Relu, bias=b)
                    seq.wait()
                    seq.did(f(lg[:], lg[:], ACT.Exp, scale=-1.0))
                if part == 2:
                    f(aex[:, j, :], ws[:, j, SP_A:SP_A + N], ACT.Exp)
                    seq.wait()
                    f(lg[:], lg[:], ACT.Ln, bias=eps[:, 2:3]).then_inc(act_sp, 1)

            def before_s(cs, co):
                if cs == 0:
                    seq.start(2, 0)
                    for part in range(3):
                        softplus(0, 0, 0, part)
                    seq.end(1)

            def body(p):
                steps = [j for j in range(2) if p.cs is not None and p.next_s(j)]
                seq.start(2 * len(steps), p.turn)
                for j in range(2):
                    gx = p.x(j) if p.cx is not None else None

                    def copy_x():
                        act.wait_ge(pe_x, gx + 1)
                        if not p.start(j):
                            act.wait_ge(dve_conv, gx)
                        nc.scalar.copy(xraw[:, HALO:], p_x[j][:]).then_inc(act_x, 1)

                    for q in range(NU if p.cs is not None else 0):
                        gs = p.s(j)
                        if q == 0:
                            act.wait_ge(dve_dt, gs + 1)
                            act.wait_ge(act_sp, gs + 1)
                        if not (p.s_start(j) and q < 2):
                            act.wait_ge(dve_h, gs * NU + (q - 1))
                        for n in range(U):
                            ins = f(da[:, q % 2, n, :], ndt[:], ACT.Exp, scale=aex[:, j, q * U + n:q * U + n + 1])
                        ins.then_inc(act_da, 1)
                        if 3 <= q < 6 and p.next_s(j):
                            softplus(*p.next_s(j), q - 3)
                        if q == 6 and p.cx is not None:
                            copy_x()
                    if p.cx is not None:
                        if p.cs is None:
                            copy_x()
                        act.wait_ge(dve_conv, gx + 1)
                        if not (p.cx == 0 and p.first):
                            act.wait_ge(pe_ss, gx - 1)
                            act.wait_ge(st_u[j], (p.i + PAIRS * p.cx) * 16)
                        f(uo[:, j, :], xc[:], ACT.Silu).then_inc(act_u, 1)
                        if p.gates0:
                            act.wait_ge(pe_g0, gx - (MT - 1))
                            if not (p.first and j == 0):
                                act.wait_ge(st_sg0, (gx - MT) * 16)
                            f(go[:], p_o[:], ACT.Silu).then_inc(act_sg0, 1)
                            if j == 0:
                                act.wait_ge(pe_f0, p.i + 1)
                                if not p.first:
                                    act.wait_ge(st_g0, p.i * 16)
                                f(xo[:], p_f[:], ACT.Silu, bias=wf[:, FW - 1:FW]).then_inc(act_f0, 1)
                        if p.gates:
                            act.wait_ge(pe_g, gx - (MT - 1))
                            if not (p.cx == 1 and p.first and j == 0):
                                act.wait_ge(st_sg, (gx - MT) * 16)
                            f(sgo[:], p_g[:], ACT.Silu).then_inc(act_sg, 1)
                            if j == 1:
                                gf = p.i + OT * (p.cx - 1)
                                act.wait_ge(pe_f, gf + 1)
                                if not (p.cx == 1 and p.first):
                                    act.wait_ge(st_g, gf * 16)
                                f(fo[:], p_f[:], ACT.Silu, bias=wf[:, FW - 1:FW]).then_inc(act_f, 1)
                seq.end(p.turns)

            def after_x(cx):
                act.wait_ge(pe_ss, MT * (cx + 1))
                if cx > 1:
                    act.wait_ge(pe_dt, MT * (cx - 1))
                    act.wait_ge(st_bc, 16 * (cx - 1))
                act.wait_ge(act_u, MT * (cx + 1))
                nc.scalar.copy(ssr, p_ss[0:SS, :])
                f(ssn[cx % 2], p_ss[0:SS, :], ACT.Square).then_inc(act_ss, 1)
                act.wait_ge(pe_ms, cx + 1)
                f(ssn[cx % 2], p_ms[0:SS, :], ACT.Sqrt, bias=eps[0:SS, 1:2]).then_inc(act_rms, 1)

            run(act, body, before_s, after_x)

        @block.vector
        def _(dve):
            v = nc.vector
            seq = Seq(dve, dve_seq)
            v.memset(eps[:, 0:1], 1e-5)
            v.memset(eps[:, 1:2], 1e-6)
            v.memset(eps[:, 2:3], 1.0).then_inc(s_eps, 1)
            dve.wait_ge(s_const, 16 * 7)
            def ln_scores(t):
                dve.wait_ge(ln_zh, t + 1)
                v.tensor_tensor(rt(0)[:, bass.ds(t, 1), :].rearrange("p a b -> p (a b)"), ps[5][0:NA, 0:E], b8t, ALU.add).then_inc(ln_h, 1)

            def ln_pair(i):
                seq.start(4, i - 1 if not isinstance(i, int) else 0)
                for j in range(2):
                    t = i * 2 + j
                    dve.wait_ge(ln_in[j], (i + 1) * 16)
                    if not isinstance(i, int):
                        dve.wait_ge(ln_norm, t - 1)
                    for h in range(2):
                        ins = v.bn_stats(st6[:, j, h, :], lnx[j][:, h * 512:(h + 1) * 512])
                    seq.did(ins)
                    seq.wait()
                    dve.sem_inc(dve_passed, 1)
                    v.bn_aggr(mv[:, j, :], st6[:, j, :, :].rearrange("p a b -> p (a b)")).then_inc(ln_var, 1)
                    dve.wait_ge(ln_std, t + 1)
                    seq.did(v.reciprocal(std[:, 2 + j:3 + j], std[:, j:j + 1]))
                    seq.wait()
                    if not isinstance(i, int):
                        dve.wait_ge(ln_tr, t - 1)
                    v.tensor_scalar(lnn[j], lnx[j], mv[:, j, 0:1], std[:, 2 + j:3 + j], ALU.subtract, ALU.mult).then_inc(ln_norm, 1)
                    if not (isinstance(i, int) and j == 0):
                        ln_scores(t - 1)
                seq.end(1 if isinstance(i, int) else TT // 2 - 1)

            ln_pair(0)
            with dve.Fori(1, TT // 2) as i:
                ln_pair(i)
            ln_scores(TT - 1)
            n_r = [0]

            def did(ins):
                ins.then_inc(r_dve, 1)
                n_r[0] += 1
                dve.wait_ge(r_dve, n_r[0])

            bc = lambda a: a.rearrange("p (a b) -> p a b", b=1).broadcast_to([NA, TT, E])
            dve.wait_ge(r_pe, 1)
            dve.wait_ge(ln_h, TT)
            did(v.tensor_copy(rt(1), ps[6][0:NA, 0:TT * E].rearrange("p (a b) -> p a b", a=TT)))
            dve.wait_ge(r_act, 2)
            v.tensor_reduce(gmx[:, 0:1], rt(2), AX.XY, ALU.max)
            did(v.tensor_reduce(gmx[:, 1:2], rt(3), AX.XY, ALU.max))
            dve.wait_ge(r_pool, 1)
            seq.start(17, 0)
            step = lambda ins: (seq.did(ins), seq.wait())
            step(v.tensor_scalar(gmx[:, 4:6], gmx[:, 2:4], 1e-6, None, ALU.max))
            step(v.reciprocal(gmx[:, 0:2], gmx[:, 4:6]))
            step(v.tensor_scalar(gmx[:, 2:4], gmx[:, 0:2], 0.5, None, ALU.mult))
            step(v.tensor_scalar(rt(0), rt(0), gmx[:, 2:3], None, ALU.mult))
            step(v.tensor_scalar(rt(1), rt(1), gmx[:, 3:4], None, ALU.mult))
            did(v.tensor_tensor(rt(3), rt(1), rt(0), ALU.add))
            step(v.tensor_reduce(r16(0), rt(3), AX.X, ALU.max))
            did(v.tensor_tensor(rt(3), rt(3), bc(r16(0)), ALU.subtract))
            dve.wait_ge(r_act, 3)
            did(v.tensor_reduce(r16(1), rt(2), AX.X, ALU.add))
            step(v.reciprocal(r16(2), r16(1)))
            did(v.tensor_tensor(rt(1), rt(2), bc(r16(2)), ALU.mult))
            for t in range(TT):
                ins = v.max(rt(4)[:, t, :], rt(1)[:, t, :])
            step(ins)
            did(v.tensor_tensor(rt(0), rt(1), rt(4)[:, :, 1:2].broadcast_to([NA, TT, E]), ALU.subtract))
            dve.wait_ge(r_dve, 8)
            step(v.tensor_scalar(rt(3), rt(3), 1.0, None, ALU.add))
            step(v.reciprocal(rt(2), rt(3)))
            step(v.tensor_tensor(rt(0), rt(1), rt(2), ALU.mult))
            step(v.tensor_reduce(r16(3), rt(0), AX.X, ALU.add))
            step(v.tensor_scalar(r16(4), r16(3), 1e-9, None, ALU.add))
            step(v.reciprocal(r16(5), r16(4)))
            step(v.tensor_tensor(rt(5), rt(0), bc(r16(5)), ALU.mult))
            step(v.tensor_copy(gmx[:, 6:7], gmx[:, 4:5]))
            step(v.tensor_copy(gmx[:, 6:7], gmx[:, 4:5]))
            seq.end(1)
            v.tensor_copy(gmx[:, 6:7], gmx[:, 4:5]).then_inc(r_dve, 2)
            dve.wait_ge(r_pe, 3)
            for h in range(2):
                zv = z_t[:, h * L:(h + 1) * L].rearrange("p (a b) -> p a b", b=2)
                pm = ps[2 + h][0:RANK, :].rearrange("p (a b) -> p a b", b=1).broadcast_to([RANK, T, 2])
                ins = v.scalar_tensor_tensor(zv, pm, 0.5, zv, ALU.mult, ALU.mult)
            ins.then_inc(r_zp, 1)

            def dt(c, k, j):
                dve.wait_ge(act_sp, k * 2 + (j + MT * c + 1))
                dve.wait_ge(ld_s[j], (k + (PAIRS * c + 1)) * 48)
                seq.wait()
                seq.did(v.scalar_tensor_tensor(ndt[:], rl[:], -1.0, lg[:], ALU.mult, ALU.subtract))
                seq.wait()
                v.scalar_tensor_tensor(dtu[:], ndt[:], -1.0, ui[:, j, :], ALU.mult, ALU.mult).then_inc(dve_dt, 1)

            def before_s(cs, co):
                if cs == 0:
                    seq.start(1, 0)
                    dt(0, 0, 0)
                    seq.end(1)

            def y_count(c):
                return MT * sum(len(u) for u in PE_UNITS[:c])

            def body(p):
                cx, cs, co = p.cx, p.cs, p.co
                units = PE_UNITS[cs] if cs is not None else ()
                carried = cs is not None and cs % HALVES > 0
                carries = cs is not None and cs % HALVES < HALVES - 1
                mine = [q for q in range(NU) if q not in units]
                per = 0
                if cs is not None:
                    per += 2 * (carried + NU + NU * U + 2 * len(mine) - 1 + 2) + sum(p.next_s(j) is not None for j in range(2))
                if cx is not None:
                    per += 2 * (1 + K_CONV)
                if co is not None:
                    per += 1
                seq.start(per, p.turn)
                for j in range(2):
                    m, ms = p.i * 2 + j, p.k * 2 + j
                    gs = p.s(j) if cs is not None else None
                    gx = p.x(j) if cx is not None else None
                    made, summed = {}, {}

                    def add_pair(q):
                        dve.wait_ge(pool_p, gs * NU + (q + 1))
                        p0, p1 = hb[:, q % RING, 0, :], hb[:, q % RING, 1, :]
                        if q == mine[0] and not p.s_start(j):
                            dve.wait_ge(dve_y, gs)
                        summed[q] = seq.did(v.tensor_tensor(yacc[:] if q == mine[0] else p0, p0, p1, ALU.add))

                    def add_on(q):
                        if q != mine[0]:
                            seq.wait(summed[q])
                            summed[q] = seq.did(v.tensor_tensor(yacc[:], yacc[:], hb[:, q % RING, 0, :], ALU.add))

                    def make(q):
                        if q - RING in units:
                            dve.wait_ge(pe_y, y_count(cs) + ms * len(units) + (units.index(q - RING) + 1))
                        if p.s_first and j == 0 and q % (NU // PB) == 0:
                            dve.wait_ge(ld_b[q // (NU // PB)], 16 * (cs + 1))
                        if q - RING in summed:
                            seq.wait(summed[q - RING])
                        w = dtu[:].rearrange("p (a t) -> p a t", a=1).broadcast_to([P, U, T])
                        made[q] = seq.did(v.tensor_tensor(hb[:, q % RING], w, bb[:, q * U:(q + 1) * U, :], ALU.mult))

                    tap = lambda k: wxx[:, j, SS + k:SS + k + 1]

                    def conv(k):
                        if k == 0:
                            seq.wait()
                            seq.did(v.tensor_scalar(xc[:], xraw[:, 0:T], tap(0), tap(K_CONV), ALU.mult, ALU.add))
                        else:
                            seq.wait(taps[-1])
                            seq.did(v.scalar_tensor_tensor(xc[:], xraw[:, k:k + T], tap(k), xc[:], ALU.mult, ALU.add))
                        taps.append(seq.n)

                    taps = []
                    if cs is not None:
                        if not p.s_start(j):
                            dve.wait_ge(dve_h, gs * NU)
                        if carried:
                            loaded = seq.did(v.tensor_scalar(st[:], states[:, bass.ds(ms, 1), :].rearrange("p a b -> p (a b)"), 1.0, None, ALU.mult))
                        dve.wait_ge(dve_dt, gs + 1)
                        if not p.s_start(j):
                            dve.wait_ge(dve_y, gs)
                        make(0)
                        for q in range(NU):
                            if q + 1 < NU:
                                make(q + 1)
                            hq = hb[:, q % RING]
                            seq.wait(max(made[q], loaded if carried else 0))
                            dve.wait_ge(act_da, gs * NU + (q + 1))
                            for n in range(U):
                                init = st[:, q * U + n:q * U + n + 1] if carried else 0.0
                                scanned = seq.did(v.tensor_tensor_scan(hq[:, n, :], da[:, q % 2, n, :], hq[:, n, :], init, ALU.mult, ALU.add))
                            if q - 2 in mine:
                                add_pair(q - 2)
                            seq.wait(scanned)
                            v.tensor_copy(st[:, q * U:(q + 1) * U], hq[:, :, T - 1:T].rearrange("p a b -> p (a b)")).then_inc(dve_h, 1)
                            if q - 2 in mine:
                                add_on(q - 2)
                        if carries:
                            dve.wait_ge(dve_h, gs * NU + NU)
                            v.tensor_scalar(states[:, bass.ds(ms, 1), :].rearrange("p a b -> p (a b)"), st[:], 1.0, None, ALU.mult)
                        if p.next_s(j):
                            dt(*p.next_s(j))
                    if cx is not None:
                        dve.wait_ge(act_x, gx + 1)
                        if not p.start(j):
                            dve.wait_ge(act_u, gx)
                            dve.wait_ge(dve_conv, gx)
                        dve.wait_ge(ld_w[j], (p.i + (PAIRS * cx + 1)) * 16)
                        if cx % HALVES == 0:
                            seq.did(v.memset(xraw[:, 0:HALO], 0.0))
                        else:
                            seq.did(v.tensor_scalar(xraw[:, 0:HALO], tails[:, bass.ds(m, 1), :].rearrange("p a b -> p (a b)"), 1.0, None, ALU.mult))
                        conv(0)
                    if NU - 2 in mine and cs is not None:
                        add_pair(NU - 2)
                    if cx is not None:
                        conv(1)
                    if cs is not None:
                        if NU - 2 in mine:
                            add_on(NU - 2)
                        add_pair(NU - 1)
                    if cx is not None:
                        conv(2)
                    if cs is not None:
                        add_on(NU - 1)
                    if cx is not None:
                        conv(3)
                        seq.wait(taps[-1])
                        v.tensor_scalar(tails[:, bass.ds(m, 1), :].rearrange("p a b -> p (a b)"), xraw[:, T:T + HALO], 1.0, None, ALU.mult).then_inc(dve_conv, 1)
                    if cs is not None:
                        seq.wait(summed[NU - 1])
                        seq.did(v.scalar_tensor_tensor(yacc[:], ui[:, j, :], ws[:, j, SP_D:SP_D + 1], yacc[:], ALU.mult, ALU.add))
                        seq.wait()
                        dve.wait_ge(pe_y, y_count(cs) + (ms + 1) * len(units))
                        seq.did(v.tensor_tensor(yacc[:], yacc[:], p_y[:], ALU.add))
                        seq.wait()
                        v.tensor_tensor(sgi[:, j, :], yacc[:], sgi[:, j, :], ALU.mult).then_inc(dve_y, 1)
                    if co is not None and j == 1:
                        go_n = p.k + OT * co
                        dve.wait_ge(pe_o, (go_n + 1) * 2)
                        dve.wait_ge(ld_r, (go_n + 1) * 32)
                        seq.did(v.tensor_tensor(go[:], p_o[:], go[:], ALU.mult))
                        seq.wait()
                        v.tensor_tensor(xo[:], xo[:], go[:], ALU.add).then_inc(dve_o, 1)
                seq.end(p.turns)

            def after_x(cx):
                dve.wait_ge(act_rms, cx + 1)
                seq.start(1, 0)
                seq.did(v.reciprocal(ssn[cx % 2], ssn[cx % 2]))
                seq.wait()
                v.tensor_tensor(ssn[cx % 2], ssn[cx % 2], ssr, ALU.mult).then_inc(dve_ssn, 1)
                seq.end(1)

            run(dve, body, before_s, after_x)

        @block.gpsimd
        def _(pool):
            pool.wait_ge(r_dve, 2)
            nc.gpsimd.partition_all_reduce(gmx[:, 2:4], gmx[:, 0:2], NA, bass.bass_isa.ReduceOp.max).then_inc(r_pool, 1)

            def body(p):
                for j in range(2 if p.cs is not None else 0):
                    for q in range(NU):
                        if p.s_first and j == 0 and q % (NU // PB) == 0:
                            pool.wait_ge(ld_c[q // (NU // PB)], 16 * (p.cs + 1))
                        pool.wait_ge(dve_h, p.s(j) * NU + (q + 1))
                        nc.gpsimd.tensor_tensor(hb[:, q % RING], hb[:, q % RING], cb[:, q * U:(q + 1) * U, :], ALU.mult).then_inc(pool_p, 1)

            run(pool, body)


_OUTS = ("out", (NC, OT, P, T))


def kernel(L0_attn_hidden_states, L0_attn_W_in, L0_attn_conv_w, L0_attn_conv_b, L0_attn_W_x, L0_attn_W_dt,
           L0_attn_b_dt, L0_attn_A_log, L0_attn_D, L0_attn_W_out, L0_ffn_W, L0_ffn_b, L0_ffn_A, L0_ffn_Bmat,
           L0_ffn_LiMEs):
    import numpy as np
    import concourse.bacc as bacc
    from concourse.bass_utils import run_bass_kernel_spmd

    def tiles(w, k):
        return w.reshape(-1, P, k, P).transpose(0, 3, 2, 1).reshape(-1, P, k * P)

    def cols(v):
        return v.reshape(-1, P, v.size // v.shape[0])

    x = L0_attn_hidden_states.reshape(TOK, H)
    f32 = x.dtype
    w_in = tiles(L0_attn_W_in, KH)
    w_dt = np.zeros((MT, P, P), f32)
    w_dt[:, :R] = L0_attn_W_dt.reshape(MT, P, R).transpose(0, 2, 1)
    b_mat = np.zeros((OT, P, P), f32)
    b_mat[:, SS:] = L0_ffn_Bmat.reshape(RANK, OT, P).transpose(1, 0, 2)
    blk = np.zeros((SS, SS), f32)
    for a, n in ((0, R), (R, N), (R + N, N)):
        blk[a:a + n, a:a + n] = 1.0 / n
    arrays = {
        "x": np.concatenate([x.reshape(TT, P, H), x.reshape(TT, P, H)[:2]]),
        "xt": x.reshape(NC, T, OT, P).transpose(0, 2, 3, 1),
        "w_in": w_in[:MT],
        "w_x": np.concatenate([L0_attn_W_x.T.reshape(MT, P, SS), cols(L0_attn_conv_w),
                               cols(L0_attn_conv_b)], axis=2),
        "w_s": np.concatenate([cols(L0_attn_A_log), cols(L0_attn_b_dt), cols(L0_attn_D), w_dt], axis=2),
        "w_g": w_in[MT:],
        "w_o": tiles(L0_attn_W_out, MT),
        "w_f": np.concatenate([tiles(L0_ffn_W, KH), b_mat, cols(L0_ffn_b)], axis=2),
        "w8": L0_ffn_W[:E].reshape(E, KH, P).transpose(2, 1, 0),
        "a_r": L0_ffn_A.reshape(KH, P, RANK).transpose(1, 0, 2),
        "lime": L0_ffn_LiMEs,
        "lime_t": L0_ffn_LiMEs.T,
        "b8": np.broadcast_to(L0_ffn_b[:E], (NA, E)),
        "ident": np.eye(P, dtype=f32),
        "blk": blk,
    }
    nc = bacc.Bacc("TRN2", target_bir_lowering=False, num_devices=1)
    arrays = {k: np.ascontiguousarray(v) for k, v in arrays.items()}
    args = [nc.dram_tensor(k, v.shape, F32, kind="ExternalInput").ap() for k, v in arrays.items()]
    out = nc.dram_tensor(_OUTS[0], _OUTS[1], F32, kind="ExternalOutput").ap()
    build(nc, *args, out)
    r = run_bass_kernel_spmd(nc, [arrays], core_ids=[0]).results[0]["out"]
    return r.transpose(0, 3, 1, 2).reshape(BATCH, L, H)
```

```python
from contextlib import ExitStack

import concourse.bass as bass
from concourse import mybir

F32 = mybir.dt.float32
ALU = mybir.AluOpType
ACT = mybir.ActivationFunctionType
AX = mybir.AxisListType

P = 128
BATCH, L, H = 2, 1024, 1024
D_IN, N, K_CONV, R = 2048, 16, 4, 64
E, RANK = 8, 32
TOK = BATCH * L
T = 512
NC = TOK // T
HALVES = L // T
KH = H // P
MT = D_IN // P
OT = H // P
SS = R + 2 * N
TT = TOK // P
LN = 4
LT = TT // LN
NA = P // 2
U = 2
NU = N // U
RING = 4
PE_UNITS = ((5,), (1, 3, 5), (1, 3, 5), (1, 3, 5))
PB = 4
PAIRS = MT // 2
WX = KH * P
WXW = SS + K_CONV + 1
SP_A, SP_B, SP_D, SP_W = 0, N, N + 1, N + 2
SPW = SP_W + P
FW = KH * P + P + 1
HALO = K_CONV - 1


class Seq:

    def __init__(self, eng, sem):
        self.eng, self.sem, self.base, self.turn, self.n = eng, sem, 0, 0, 0

    def start(self, per, turn):
        self.per, self.turn, self.n = per, turn, 0

    def end(self, turns):
        assert self.n == self.per, (self.n, self.per)
        self.base += self.per * turns

    def did(self, ins):
        ins.then_inc(self.sem, 1)
        self.n += 1
        return self.n

    def wait(self, n=None):
        n = self.n if n is None else n
        self.eng.wait_ge(self.sem, self.turn * self.per + (self.base + n))


def build(nc, x, xt, w_in, w_x, w_s, w_g, w_o, w_f, w8, a_r, lime, lime_t, b8, ident, blk, out):
    ctx = ExitStack()
    with ctx:
        sb = lambda name, shape: ctx.enter_context(nc.sbuf_tensor(name, shape, F32))
        sem = lambda name: ctx.enter_context(nc.semaphore(name))
        dram = lambda name, shape: nc.dram_tensor(name, shape, F32, kind="Internal").ap()

        xn_d = dram("xn_d", (TT, P, KH, P))
        zp_d = dram("zp_d", (NC, RANK, T))
        u_d = dram("u_d", (NC, MT, P, T))
        sg_d = dram("sg_d", (NC, MT, P, T))
        g_d = dram("g_d", (NC, OT, P, T))
        y_d = dram("y_d", (NC, MT, P, T))
        bc_d = dram("bc_d", (NC, 2, N * T))

        idt = sb("idt", [P, P])
        blkt = sb("blkt", [SS, SS])
        eps = sb("eps", [P, 3])
        bb = sb("bb", [P, N, T])
        cb = sb("cb", [P, N, T])
        hb = sb("hb", [P, RING, U, T])
        da = sb("da", [P, 2, U, T])
        yb = sb("yb", [P, MT, T])
        xn1 = sb("xn1", [P, KH, T])
        xn0 = yb[:, 0:KH, :]
        wx = sb("wx", [P, 2, WX])
        wxx = sb("wxx", [P, 2, WXW])
        wg = sb("wg", [P, 2, WX])
        wf = sb("wf", [P, FW])
        wo = sb("wo", [P, MT * P])
        ws = sb("ws", [P, 2, SPW])
        xraw = sb("xraw", [P, T + HALO])
        tails = sb("tails", [P, MT, HALO])
        xc = sb("xc", [P, T])
        uo = sb("uo", [P, 2, T])
        sgo = sb("sgo", [P, T])
        fo = sb("fo", [P, T])
        ui = sb("ui", [P, 2, T])
        sgi = sb("sgi", [P, 2, T])
        rl = sb("rl", [P, T])
        lg = sb("lg", [P, T])
        ndt = sb("ndt", [P, T])
        dtu = sb("dtu", [P, T])
        aex = sb("aex", [P, 2, N])
        st = sb("st", [P, N])
        states = sb("states", [P, MT, N])
        yacc = sb("yacc", [P, T])
        xo = sb("xo", [P, T])
        go = sb("go", [P, T])
        ssn_zp = sb("ssn_zp", [P, 2, T])
        ssn, zp = ([ssn_zp[a:b, h, :] for h in range(2)] for a, b in ((0, SS), (SS, P)))
        ssr = xc[0:SS, :]
        ps = [ctx.enter_context(nc.psum_tensor(f"ps{k}", [P, T], F32)) for k in range(8)]
        p_x, (p_g, p_dt, p_ss, p_o, p_f, p_y) = (ps[0], ps[6]), (*ps[1:6], ps[7])
        p_ms = p_ss

        flat = lambda t: t[:].rearrange("p a b -> p (a b)")
        lnx = [bb[:, 2 * j:2 * j + 2, :].rearrange("p a b -> p (a b)") for j in range(LN)]
        lnn = [bb[:, 8 + 2 * j:10 + 2 * j, :].rearrange("p a b -> p (a b)") for j in range(2)]
        lnt = [bb[:, 12 + 2 * j:14 + 2 * j, :].rearrange("p a b -> p (a b)").rearrange("p (k t) -> p k t", k=KH) for j in range(2)]
        z_t = cb[0:RANK, 0:TOK // T, :].rearrange("p a b -> p (a b)")
        w8t = cb[:, 4, 0:KH * E].rearrange("p (k e) -> p k e", k=KH)
        art = cb[:, 5, 0:KH * RANK].rearrange("p (k e) -> p k e", k=KH)
        limet = cb[0:E, 6, 0:RANK]
        limett = cb[0:RANK, 6, RANK:RANK + E]
        b8t = cb[0:NA, 7, 0:E]
        w_t = cb[0:E, 8:10, :].rearrange("p a b -> p (a b)")
        rt = lambda k: cb[0:NA, 10 + k // 4, (k % 4) * TT * E:(k % 4 + 1) * TT * E].rearrange("p (a b) -> p a b", a=TT)
        small = cb[:, 14, :]
        st6 = small[:, 0:24].rearrange("p (j a b) -> p j a b", j=2, a=2)
        mv = small[:, 24:28].rearrange("p (j a) -> p j a", j=2)
        std = small[:, 28:32]
        gmx = small[0:NA, 40:48]
        ln_sc = [ps[5][0:NA, 0:E], ps[7][0:NA, 0:E]]
        r16 = lambda k: small[0:NA, 64 + 16 * k:80 + 16 * k]

        s_const, s_eps = sem("s_const"), sem("s_eps")
        ln_in = [sem(f"ln_in{j}") for j in range(LN)]
        ln_var, ln_std, ln_norm = sem("ln_var"), sem("ln_std"), sem("ln_norm")
        ln_tr, ln_tc, ln_zh = sem("ln_tr"), sem("ln_tc"), sem("ln_zh")
        ln_z, ln_h, ln_st, st_zp = sem("ln_z"), sem("ln_h"), [sem("ln_st0"), sem("ln_st1")], sem("st_zp")
        r_pe, r_act, r_dve, r_pool, r_zp = sem("r_pe"), sem("r_act"), sem("r_dve"), sem("r_pool"), sem("r_zp")
        ld_x = [sem("ld_x0"), sem("ld_x1")]
        ld_w = [sem("ld_w0"), sem("ld_w1")]
        ld_g = [sem("ld_g0"), sem("ld_g1")]
        ld_s = [sem("ld_s0"), sem("ld_s1")]
        ld_sg = [sem("ld_sg0"), sem("ld_sg1")]
        ld_o = [sem("ld_o0"), sem("ld_o1")]
        ld_f, ld_r, ld_xn = (sem(n) for n in ("ld_f", "ld_r", "ld_xn"))
        ld_y = [sem("ld_y0"), sem("ld_y1")]
        ld_b = [sem(f"ld_b{n}") for n in range(PB)]
        ld_c = [sem(f"ld_c{n}") for n in range(PB)]
        st_u = [sem("st_u0"), sem("st_u1")]
        st_sg, st_g, st_y, st_o, st_bc = (sem(n) for n in ("st_sg", "st_g", "st_y", "st_o", "st_bc"))
        pe_x, act_x, dve_conv, act_u, pe_ss = (sem(n) for n in ("pe_x", "act_x", "dve_conv", "act_u", "pe_ss"))
        pe_g, act_sg, pe_f, act_f = (sem(n) for n in ("pe_g", "act_sg", "pe_f", "act_f"))
        act_ss, pe_ms, act_rms, dve_ssn = (sem(n) for n in ("act_ss", "pe_ms", "act_rms", "dve_ssn"))
        pe_g0, act_sg0, st_sg0, pe_f0, act_f0, st_g0 = (
            sem(n) for n in ("pe_g0", "act_sg0", "st_sg0", "pe_f0", "act_f0", "st_g0"))
        pe_dt, act_sp, dve_dt, act_da, dve_h, pool_p, dve_y = (
            sem(n) for n in ("pe_dt", "act_sp", "dve_dt", "act_da", "dve_h", "pool_p", "dve_y"))
        pe_y, dve_ud = sem("pe_y"), sem("dve_ud")
        pe_o, dve_o = sem("pe_o"), sem("dve_o")
        sp_passed, dve_passed = sem("sp_passed"), sem("dve_passed")
        act_seq, dve_seq = sem("act_seq"), sem("dve_seq")

        block = ctx.enter_context(nc.Block())

        def ln_run(eng, turn):
            turn(0)
            with eng.Fori(1, LT - 1) as i:
                turn(i)
            turn(LT - 1)

        ln_first = lambda i, j, n=1: isinstance(i, int) and i == 0 and j < n
        ln_last = lambda i, j=LN - 1: isinstance(i, int) and i == LT - 1 and j == LN - 1

        chunk = lambda c: c if 0 <= c < NC else None

        class Pair:

            def __init__(self, i, s):
                self.i, self.turns, self.turn = i, 1, 0
                self.cx = chunk(s)
                self.k, d = (PAIRS - 1, 1) if isinstance(i, int) and i == 0 else (i - 1, 0)
                self.cs, self.co = chunk(s - 1 - d), chunk(s - 2 - d)
                if not isinstance(i, int):
                    self.turns, self.turn = PAIRS - 3, i - 2
                self.first, self.last = (isinstance(i, int) and i == n for n in (0, PAIRS - 1))
                self.s_first, self.s_last = (isinstance(self.k, int) and self.k == n for n in (0, PAIRS - 1))
                self.gates = self.cx is not None and self.cx > 0
                self.gates0 = self.cx == 1

            def x(self, j):
                return self.i * 2 + (j + MT * self.cx)

            def s(self, j):
                return self.k * 2 + (j + MT * self.cs)

            def next_s(self, j):
                if self.s_last and j == 1:
                    return (self.cs + 1, 0, 0) if self.cs + 1 < NC else None
                return self.cs, self.k + j, 1 - j

            def start(self, j=0):
                return self.cx == 0 and self.first and j == 0

            def s_start(self, j=0):
                return self.cs == 0 and self.s_first and j == 0

        def run(eng, body, before_s=None, after_x=None, before_x=None):
            for s in range(NC + 3):
                if before_x:
                    before_x(chunk(s), chunk(s - 2))
                body(Pair(0, s))
                if s == NC + 2:
                    break
                if before_s:
                    before_s(chunk(s - 1), chunk(s - 2))
                body(Pair(1, s))
                with eng.Fori(2, PAIRS - 1) as i:
                    body(Pair(i, s))
                body(Pair(PAIRS - 1, s))
                if after_x and chunk(s) is not None:
                    after_x(s)

        @block.sync
        def _(sp):
            def wait(s, count):
                sp.wait_ge(s, count)
                if not isinstance(count, int):
                    sp.sem_inc(sp_passed, 1)

            for dst, src in ((idt[:], ident), (blkt[:], blk), (w8t, w8), (art, a_r), (limet, lime),
                             (limett, lime_t), (b8t, b8)):
                sp.dma_start(dst, src).then_inc(s_const, 16)

            def ln_load(t, j):
                sp.dma_start(lnx[j], x[t]).then_inc(ln_in[j], 16)

            def ln_store(t, j):
                wait(ln_tc, t + 1)
                sp.dma_start(xn_d[t], lnt[j % 2]).then_inc(ln_st[j % 2], 16)

            def ln_turn(i):
                for j in range(LN):
                    t = i * LN + j
                    if not ln_last(i):
                        wait(ln_norm, t + 1)
                        ln_load(t + LN, j)
                    if not ln_first(i, j):
                        ln_store(t - 1, j - 1)

            for j in range(LN):
                ln_load(j, j)
            ln_run(sp, ln_turn)
            ln_store(TT - 1, 1)
            for h in range(2):
                wait(ln_st[h], 16 * TT // 2)
            wait(r_zp, 1)
            for c in range(NC):
                sp.dma_start(zp_d[c], z_t[:, c * T:(c + 1) * T]).then_inc(st_zp, 16)
            wait(st_zp, 16 * NC)

            def load_x(m, j):
                sp.dma_start(wx[:, j, :], w_in[m]).then_inc(ld_x[j], 16)

            def load_w(m, j, gates):
                sp.dma_start(wxx[:, j, :], w_x[m]).then_inc(ld_w[j], 16)
                if gates:
                    sp.dma_start(wg[:, j, :], w_g[m]).then_inc(ld_g[j], 16)

            def load_s(c, m, j):
                sp.dma_start(ws[:, j, :], w_s[m]).then_inc(ld_s[j], 16)
                sp.dma_start(ui[:, j, :], u_d[c, m]).then_inc(ld_s[j], 16)

            def load_gate(c, m, j):
                sp.dma_start(sgi[:, j, :], sg_d[c, m]).then_inc(ld_sg[j], 16)

            def load_o(o, h):
                w = MT * P // 2
                sp.dma_start(wo[:, h * w:(h + 1) * w], w_o[o, :, h * w:(h + 1) * w]).then_inc(ld_o[h], 16)

            def load_bc(c, n):
                a, b = n * N * T // PB, (n + 1) * N * T // PB
                sp.dma_start(flat(bb)[:, a:b], bc_d[c, 0:1, a:b].partition_broadcast(P)).then_inc(ld_b[n], 16)
                if c > 0:
                    wait(pool_p, NU * (MT * c - 1) + NU // PB * (n + 1))
                sp.dma_start(flat(cb)[:, a:b], bc_d[c, 1:2, a:b].partition_broadcast(P)).then_inc(ld_c[n], 16)

            def load_xn(cx):
                xn = xn1 if cx > 0 else xn0
                for r in range(T // P):
                    sp.dma_start(xn[:, :, r * P:(r + 1) * P], xn_d[cx * (T // P) + r]).then_inc(ld_xn, 16)
                sp.dma_start(zp[cx % 2], zp_d[cx]).then_inc(ld_xn, 16)

            def load_y(co, h):
                m = MT // 2 * h
                wait(st_y, 16 * (MT * co + MT // 2 * (h + 1)))
                sp.dma_start(yb[:, m:m + MT // 2, :], y_d[co, m:m + MT // 2].rearrange("m p t -> p m t")).then_inc(ld_y[h], 16)

            def before_x(cx, co):
                if cx == 0:
                    load_x(0, 0)
                    load_w(0, 0, False)
                    load_xn(0)
                    load_x(1, 1)
                if co == 0:
                    wait(pe_g0, MT)
                    wait(pe_f0, OT)
                    load_o(0, 0)
                    load_y(0, 0)

            def before_s(cs, co):
                if cs == 0:
                    wait(st_sg0, 16 * 1)
                    load_s(0, 0, 0)
                    load_gate(0, 0, 0)
                    for n in range(PB):
                        load_bc(0, n)
                    load_s(0, 1, 1)
                if cs is None:
                    load_xn(1)
                if co is not None:
                    wait(st_g if co else st_g0, 16 * OT * max(co, 1))
                    if co > 0:
                        wait(pe_o, 2 * OT * co)
                    load_o(0, 1)
                    load_y(co, 1)

            def after_x(cx):
                if cx + 1 < NC:
                    if cx > 0:
                        wait(pe_x, MT * (cx + 1))
                        wait(pe_g, MT * cx)
                        wait(pe_f, OT * cx)
                        load_xn(cx + 1)
                        wait(act_f, OT * cx)
                    load_x(0, 0)
                    wait(pe_ss, MT * (cx + 1) - 1)
                    wait(dve_conv, MT * (cx + 1) - 1)
                    load_w(0, 0, True)
                    wait(pe_x, MT * (cx + 1))
                    load_x(1, 1)
                    sp.dma_start(wf[:], w_f[0]).then_inc(ld_f, 16)
                wait(dve_ssn, cx + 1)
                sp.dma_start(bc_d[cx].rearrange("a (n t) -> (a n) t", n=N), ssn_zp[R:SS, cx % 2, :]).then_inc(st_bc, 16)
                wait(st_bc, 16 * (cx + 1))
                for j in range(2):
                    wait(st_u[j], 16 * PAIRS * (cx + 1))
                if cx > 0:
                    wait(st_sg, 16 * MT * cx)

            def body(p):
                for j in range(2):
                    if p.cs is not None:
                        nxt = p.next_s(j)
                        if nxt:
                            c, k, nj = nxt
                            if not p.s_start(j):
                                wait(st_y, p.s(j) * 16)
                            if c == 0:
                                wait(st_sg0, (k * 2 + (nj + 1)) * 16)
                            load_gate(c, k * 2 + nj, nj)
                    if p.cx is not None:
                        gx = p.x(j)
                        if not p.last:
                            wait(pe_x, gx + 1)
                            load_x(p.i * 2 + (j + 2), j)
                        if not (p.last and j == 1):
                            if not p.start(j):
                                wait(pe_ss, gx)
                                wait(dve_conv, gx)
                                if p.cx > 1 or p.cx == 1 and not (p.first and j == 0):
                                    wait(pe_g, gx - MT)
                            load_w(p.i * 2 + (j + 1), 1 - j, p.gates)
                    if p.cs is not None and not (p.s_last and p.cs + 1 == NC):
                        wait(dve_ud, p.s(j) + 1)
                        if p.s_last:
                            load_s(p.cs + 1, j, j)
                        else:
                            load_s(p.cs, (p.k + 1) * 2 + j, j)
                    if p.cs is not None and p.s_last and j == 1 and nxt:
                        for n in range(PB):
                            wait(dve_h, NU * (MT * nxt[0] - 1) + NU // PB * (n + 1))
                            load_bc(nxt[0], n)
                    if p.cx is not None:
                        if p.gates0:
                            wait(act_sg0, gx - (MT - 1))
                            sp.dma_start(sg_d[0, p.i * 2 + j], go[:]).then_inc(st_sg0, 16)
                            if j == 0:
                                wait(act_f0, p.i + 1)
                                sp.dma_start(g_d[0, p.i], xo[:]).then_inc(st_g0, 16)
                        wait(act_u, gx + 1)
                        sp.dma_start(u_d[p.cx, p.i * 2 + j], uo[:, j, :]).then_inc(st_u[j], 16)
                        if p.gates:
                            wait(act_sg, gx - (MT - 1))
                            sp.dma_start(sg_d[p.cx, p.i * 2 + j], sgo[:]).then_inc(st_sg, 16)
                            if j == 1:
                                wait(act_f, p.i + (OT * (p.cx - 1) + 1))
                                sp.dma_start(g_d[p.cx, p.i], fo[:]).then_inc(st_g, 16)
                                if not p.last:
                                    sp.dma_start(wf[:], w_f[p.i + 1]).then_inc(ld_f, 16)
                    if p.co is not None:
                        n_o = p.k + OT * p.co
                        if j == 0:
                            if p.co > 0 or not p.s_first:
                                wait(st_o, n_o * 16)
                            sp.dma_start(xo[:], xt[p.co, p.k]).then_inc(ld_r, 16)
                            sp.dma_start(go[:], g_d[p.co, p.k]).then_inc(ld_r, 16)
                        if j == 1:
                            wait(dve_o, n_o + 1)
                            sp.dma_start(out[p.co, p.k], xo[:]).then_inc(st_o, 16)
                    if p.cs is not None:
                        wait(dve_y, p.s(j) + 1)
                        sp.dma_start(y_d[p.cs, p.k * 2 + j], sgi[:, j, :]).then_inc(st_y, 16)
                    if p.co is not None:
                        if not p.s_last:
                            wait(pe_o, n_o * 2 + (j + 1))
                            load_o(p.k + 1, j)
                        elif j == 0 and p.co + 1 < NC:
                            wait(pe_o, n_o * 2 + 1)
                            load_o(0, 0)
                            load_y(p.co + 1, 0)

            run(sp, body, before_s, after_x, before_x)
            sp.wait_ge(st_o, 16 * OT * NC)

        @block.tensor
        def _(pe):
            mm = nc.tensor.matmul

            pe.wait_ge(s_const, 16 * 7)
            def ln_z_h(t, j):
                pe.wait_ge(ln_tc, t + 1)
                if not (isinstance(t, int) and t == 0):
                    pe.wait_ge(ln_z, t)
                if not (isinstance(t, int) and t < 2):
                    pe.wait_ge(ln_h, t - 1)
                for k in range(KH):
                    mm(ps[4][0:RANK, 0:P], art[:, k, :], lnt[j][:, k, :], start=(k == 0), stop=(k == KH - 1))
                for k in range(KH):
                    ins = mm(ln_sc[j], lnt[j][:, k, 1:P:2], w8t[:, k, :], start=(k == 0), stop=(k == KH - 1))
                ins.then_inc(ln_zh, 1)

            def ln_turn(i):
                for j in range(LN):
                    t = i * LN + j
                    pe.wait_ge(ln_norm, t + 1)
                    if not ln_first(i, j, 2):
                        pe.wait_ge(ln_tc, t - 1)
                    for k in range(KH):
                        ins = nc.tensor.transpose(ps[2 * (j % 2) + k // 4][:, (k % 4) * P:(k % 4 + 1) * P],
                                                  lnn[j % 2][:, k * P:(k + 1) * P], idt[:])
                    ins.then_inc(ln_tr, 1)
                    if not ln_first(i, j):
                        ln_z_h(t - 1, 1 - j % 2)

            ln_run(pe, ln_turn)
            ln_z_h(TT - 1, 1)
            pe.wait_ge(ln_z, TT)
            for t in range(TT):
                ins = mm(ps[6][0:NA, t * E:(t + 1) * E], z_t[:, t * P + 1:(t + 1) * P:2], limett, start=True, stop=True)
            ins.then_inc(r_pe, 1)
            pe.wait_ge(r_dve, 10)
            for t in range(TT):
                ins = nc.tensor.transpose(ps[t // 8][0:E, (t % 8) * NA:(t % 8 + 1) * NA], rt(5)[:, t, :], idt[0:NA, 0:NA])
            ins.then_inc(r_pe, 1)
            pe.wait_ge(r_act, 4)
            for h in range(2):
                ins = mm(ps[2 + h][0:RANK, :], limet, w_t[:, h * T:(h + 1) * T], start=True, stop=True)
            ins.then_inc(r_pe, 1)

            pe.wait_ge(r_zp, 1)

            def before_x(cx, co):
                if cx is not None:
                    pe.wait_ge(ld_xn, 16 * (T // P + 1) * (cx + 1))

            def dt_product(c, k, j):
                pe.wait_ge(ld_s[j], (k + (PAIRS * c + 1)) * 32)
                if isinstance(k, int) and k == 0 and j == 0:
                    pe.wait_ge(dve_ssn, c + 1)
                if not (c == 0 and isinstance(k, int) and k == 0 and j == 0):
                    pe.wait_ge(act_sp, k * 2 + (j + MT * c))
                mm(p_dt[:], ws[0:R, j, SP_W:SPW], ssn[c % 2][0:R, :], start=True, stop=True).then_inc(pe_dt, 1)

            def before_s(cs, co):
                if cs == 0:
                    dt_product(0, 0, 0)

            def add_up(p, j, qs):
                units = PE_UNITS[p.cs]
                for q in qs:
                    if q not in units:
                        continue
                    pe.wait_ge(pool_p, p.s(j) * NU + (q + 1))
                    if q == units[0] and not p.s_start(j):
                        pe.wait_ge(dve_y, p.s(j))
                    for n in range(U):
                        ins = mm(p_y[:], idt[:], hb[:, q % RING, n, :], start=(q == units[0] and n == 0),
                                 stop=(q == units[-1] and n == U - 1))
                    ins.then_inc(pe_y, 1)

            def project(bank, w, src, part):
                for k in range(KH // 2 * part, KH // 2 * (part + 1)):
                    ins = mm(bank[:], w[:, k * P:(k + 1) * P], src[:, k, :], start=(k == 0), stop=(k == KH - 1))
                return ins

            def feed_forward(src, z, part):
                for k in range(KH // 2 * part, KH // 2 * (part + 1)):
                    mm(p_f[:], wf[:, k * P:(k + 1) * P], src[:, k, :], start=(k == 0), stop=False)
                if part == 1:
                    return mm(p_f[:], wf[SS:P, KH * P:KH * P + P], z, start=False, stop=True)

            def quarter(p, r):
                n_o = p.k + OT * p.co
                if r % 2 == 0:
                    pe.wait_ge(ld_o[r // 2], (n_o + 1) * 16)
                    if p.s_first:
                        pe.wait_ge(ld_y[r // 2], 16 * (p.co + 1))
                if r == 0 and p.co == 0 and p.s_first:
                    pe.wait_ge(act_sg0, MT)
                elif r == 0:
                    pe.wait_ge(dve_o, n_o)
                for k in range(MT // 4 * r, MT // 4 * (r + 1)):
                    ins = mm(p_o[:], wo[:, k * P:(k + 1) * P], yb[:, k, :], start=(k == 0), stop=(k == MT - 1))
                if r % 2 == 1:
                    ins.then_inc(pe_o, 1)

            def body(p):
                for j in range(2):
                    def sums(*qs):
                        if p.cs is not None:
                            add_up(p, j, qs)

                    if p.cx is not None:
                        gx = p.x(j)
                        xn = xn1 if p.cx > 0 else xn0
                        pe.wait_ge(ld_x[j], (p.i + (PAIRS * p.cx + 1)) * 16)
                        if not (p.cx == 0 and p.first):
                            pe.wait_ge(act_x, gx - 1)
                        project(p_x[j], wx[:, j, :], xn, 0)
                        project(p_x[j], wx[:, j, :], xn, 1).then_inc(pe_x, 1)
                    sums(0)
                    if p.cs is not None and p.next_s(j):
                        dt_product(*p.next_s(j))
                    if p.cx is not None:
                        if not (p.first and j == 0):
                            pe.wait_ge(act_u, gx)
                            if p.first and j == 1 and p.cx > 0:
                                pe.wait_ge(act_ss, p.cx)
                            pe.wait_ge(ld_w[1 - j], (p.i + (PAIRS * p.cx + j)) * 16)
                            mm(p_ss[0:SS, :], wxx[:, 1 - j, 0:SS], uo[:, 1 - j, :],
                               start=(p.first and j == 1), stop=False).then_inc(pe_ss, 1)
                    if p.gates0:
                        pe.wait_ge(ld_g[j], (p.i + 1) * 16)
                        if not (p.first and j == 0):
                            pe.wait_ge(act_sg0, gx - MT)
                        project(p_o, wg[:, j, :], xn0, 0)
                        project(p_o, wg[:, j, :], xn0, 1).then_inc(pe_g0, 1)
                        if j == 0:
                            sums(1)
                            pe.wait_ge(ld_f, (p.i + 1) * 16)
                            if not p.first:
                                pe.wait_ge(act_f, p.i)
                            feed_forward(xn0, zp[0], 0)
                            feed_forward(xn0, zp[0], 1).then_inc(pe_f0, 1)
                    if p.gates:
                        pe.wait_ge(ld_g[j], (p.i + (PAIRS * (p.cx - 1) + 1)) * 16)
                        if not (p.cx == 1 and p.first and j == 0):
                            pe.wait_ge(act_sg, gx - MT)
                        project(p_g, wg[:, j, :], xn, 0)
                    if p.gates:
                        project(p_g, wg[:, j, :], xn, 1).then_inc(pe_g, 1)
                    sums(*(2,) if p.gates0 and j == 0 else (1, 2))
                    for part in range(2):
                        if p.gates and j == 1:
                            gf = p.i + OT * (p.cx - 1)
                            if part == 0:
                                pe.wait_ge(ld_f, (gf + 1) * 16)
                                if p.gates0:
                                    pe.wait_ge(act_f0, p.i + 1)
                                else:
                                    pe.wait_ge(act_f, gf)
                            ins = feed_forward(xn, zp[p.cx % 2], part)
                            if part == 1:
                                ins.then_inc(pe_f, 1)
                        elif p.co is not None and j == 0:
                            quarter(p, part)
                        sums(3 + part)
                    if p.co is not None:
                        quarter(p, 2 + j)
                    sums(5, 6)

            def after_x(cx):
                pe.wait_ge(act_u, MT * (cx + 1))
                pe.wait_ge(ld_w[1], PAIRS * (cx + 1) * 16)
                mm(p_ss[0:SS, :], wxx[:, 1, 0:SS], uo[:, 1, :], start=False, stop=True).then_inc(pe_ss, 1)
                pe.wait_ge(act_ss, cx + 1)
                mm(p_ms[0:SS, :], blkt[:], ssn[cx % 2], start=True, stop=True).then_inc(pe_ms, 1)

            run(pe, body, before_s, after_x, before_x)

        @block.scalar
        def _(act):
            seq = Seq(act, act_seq)
            f = nc.scalar.activation
            act.wait_ge(s_eps, 1)
            def ln_copy_z(t):
                act.wait_ge(ln_zh, t + 1)
                nc.scalar.copy(z_t[:, bass.ds(t * P, P)], ps[4][0:RANK, 0:P]).then_inc(ln_z, 1)

            def ln_root(t, j):
                act.wait_ge(ln_var, t + 1)
                f(std[:, j:j + 1], mv[:, j, 1:2], ACT.Sqrt, bias=eps[:, 0:1]).then_inc(ln_std, 1)

            def ln_turn(i):
                for j in range(LN):
                    t = i * LN + j
                    if not ln_last(i, j):
                        ln_root(t + 1, 1 - j % 2)
                    act.wait_ge(ln_tr, t + 1)
                    if not ln_first(i, j, 2):
                        act.wait_ge(ln_st[j % 2], (i * 2 + j // 2) * 16)
                        act.wait_ge(ln_zh, t - 1)
                    for h in range(2):
                        ins = nc.scalar.copy(lnt[j % 2][:, 4 * h:4 * h + 4, :],
                                             ps[2 * (j % 2) + h][:].rearrange("p (a b) -> p a b", a=4))
                    ins.then_inc(ln_tc, 1)
                    if not ln_first(i, j):
                        ln_copy_z(t - 1)

            ln_root(0, 0)
            ln_run(act, ln_turn)
            ln_copy_z(TT - 1)
            act.wait_ge(r_dve, 1)
            f(rt(2), rt(0), ACT.Abs).then_inc(r_act, 1)
            f(rt(3), rt(1), ACT.Abs).then_inc(r_act, 1)
            act.wait_ge(r_dve, 4)
            f(rt(2), rt(3), ACT.Exp).then_inc(r_act, 1)
            act.wait_ge(r_dve, 7)
            f(rt(3), rt(0), ACT.Exp, scale=-2.0).then_inc(r_dve, 1)
            act.wait_ge(r_pe, 2)
            for h in range(2):
                ins = nc.scalar.copy(w_t[:, h * T:(h + 1) * T], ps[h][0:E, :])
            ins.then_inc(r_act, 1)

            def softplus(c, k, j, part):
                b = ws[:, j, SP_B:SP_B + 1]
                if part == 0:
                    act.wait_ge(pe_dt, k * 2 + (j + MT * c + 1))
                    act.wait_ge(ld_s[j], (k + (PAIRS * c + 1)) * 32)
                    if not (c == 0 and isinstance(k, int) and k == 0 and j == 0):
                        act.wait_ge(dve_dt, k * 2 + (j + MT * c))
                    seq.did(f(lg[:], p_dt[:], ACT.Abs, bias=b))
                if part == 1:
                    f(rl[:], p_dt[:], ACT.Relu, bias=b)
                    seq.wait()
                    seq.did(f(lg[:], lg[:], ACT.Exp, scale=-1.0))
                if part == 2:
                    f(aex[:, j, :], ws[:, j, SP_A:SP_A + N], ACT.Exp)
                    seq.wait()
                    f(lg[:], lg[:], ACT.Ln, bias=eps[:, 2:3]).then_inc(act_sp, 1)

            def before_s(cs, co):
                if cs == 0:
                    seq.start(2, 0)
                    for part in range(3):
                        softplus(0, 0, 0, part)
                    seq.end(1)

            def body(p):
                steps = [j for j in range(2) if p.cs is not None and p.next_s(j)]
                if p.cs is not None:
                    nc.scalar.preload_act_table_set("natural_log_exp_and_others")
                seq.start(2 * len(steps), p.turn)
                for j in range(2):
                    gx = p.x(j) if p.cx is not None else None

                    def copy_x():
                        act.wait_ge(pe_x, gx + 1)
                        if not p.start(j):
                            act.wait_ge(dve_conv, gx)
                        nc.scalar.copy(xraw[:, HALO:], p_x[j][:]).then_inc(act_x, 1)

                    for q in range(NU if p.cs is not None else 0):
                        gs = p.s(j)
                        if q == 0:
                            act.wait_ge(dve_dt, gs + 1)
                            act.wait_ge(act_sp, gs + 1)
                        if not (p.s_start(j) and q < 2):
                            act.wait_ge(dve_h, gs * NU + (q - 1))
                        for n in range(U):
                            ins = f(da[:, q % 2, n, :], ndt[:], ACT.Exp, scale=aex[:, j, q * U + n:q * U + n + 1])
                        ins.then_inc(act_da, 1)
                        if 3 <= q < 6 and p.next_s(j):
                            softplus(*p.next_s(j), q - 3)
                        if q == 6 and p.cx is not None:
                            copy_x()
                    if p.cx is not None:
                        if p.cs is None:
                            copy_x()
                        act.wait_ge(dve_conv, gx + 1)
                        if not (p.cx == 0 and p.first):
                            act.wait_ge(pe_ss, gx - 1)
                            act.wait_ge(st_u[j], (p.i + PAIRS * p.cx) * 16)
                        f(uo[:, j, :], xc[:], ACT.Silu).then_inc(act_u, 1)
                        if p.gates0:
                            act.wait_ge(pe_g0, gx - (MT - 1))
                            if not (p.first and j == 0):
                                act.wait_ge(st_sg0, (gx - MT) * 16)
                            f(go[:], p_o[:], ACT.Silu).then_inc(act_sg0, 1)
                            if j == 0:
                                act.wait_ge(pe_f0, p.i + 1)
                                if not p.first:
                                    act.wait_ge(st_g0, p.i * 16)
                                f(xo[:], p_f[:], ACT.Silu, bias=wf[:, FW - 1:FW]).then_inc(act_f0, 1)
                        if p.gates:
                            act.wait_ge(pe_g, gx - (MT - 1))
                            if not (p.cx == 1 and p.first and j == 0):
                                act.wait_ge(st_sg, (gx - MT) * 16)
                            f(sgo[:], p_g[:], ACT.Silu).then_inc(act_sg, 1)
                            if j == 1:
                                gf = p.i + OT * (p.cx - 1)
                                act.wait_ge(pe_f, gf + 1)
                                if not (p.cx == 1 and p.first):
                                    act.wait_ge(st_g, gf * 16)
                                f(fo[:], p_f[:], ACT.Silu, bias=wf[:, FW - 1:FW]).then_inc(act_f, 1)
                    if j == 0 and p.cs is not None and p.cx is not None:
                        nc.scalar.preload_act_table_set("natural_log_exp_and_others")
                seq.end(p.turns)

            def after_x(cx):
                act.wait_ge(pe_ss, MT * (cx + 1))
                if cx > 1:
                    act.wait_ge(pe_dt, MT * (cx - 1))
                    act.wait_ge(st_bc, 16 * (cx - 1))
                act.wait_ge(act_u, MT * (cx + 1))
                nc.scalar.copy(ssr, p_ss[0:SS, :])
                f(ssn[cx % 2], p_ss[0:SS, :], ACT.Square).then_inc(act_ss, 1)
                act.wait_ge(pe_ms, cx + 1)
                f(ssn[cx % 2], p_ms[0:SS, :], ACT.Sqrt, bias=eps[0:SS, 1:2]).then_inc(act_rms, 1)

            run(act, body, before_s, after_x)

        @block.vector
        def _(dve):
            v = nc.vector
            seq = Seq(dve, dve_seq)
            v.memset(eps[:, 0:1], 1e-5)
            v.memset(eps[:, 1:2], 1e-6)
            v.memset(eps[:, 2:3], 1.0).then_inc(s_eps, 1)
            dve.wait_ge(s_const, 16 * 7)
            def ln_scores(t, j):
                dve.wait_ge(ln_zh, t + 1)
                v.tensor_tensor(rt(0)[:, bass.ds(t, 1), :].rearrange("p a b -> p (a b)"), ln_sc[j % 2], b8t, ALU.add).then_inc(ln_h, 1)

            def ln_stats(t, turn, j):
                dve.wait_ge(ln_in[j], (turn + 1) * 16)
                if not (isinstance(t, int) and t < 2):
                    dve.wait_ge(ln_norm, t - 1)
                for h in range(2):
                    ins = v.bn_stats(st6[:, j % 2, h, :], lnx[j][:, h * 512:(h + 1) * 512])
                seq.did(ins)
                seq.wait()
                dve.sem_inc(dve_passed, 1)
                v.bn_aggr(mv[:, j % 2, :], st6[:, j % 2, :, :].rearrange("p a b -> p (a b)")).then_inc(ln_var, 1)

            def ln_turn(i):
                inner = not isinstance(i, int)
                seq.start(2 * LN - ln_last(i), i - 1 if inner else 0)
                for j in range(LN):
                    t, c = i * LN + j, j % 2
                    if not ln_last(i, j):
                        ln_stats(t + 1, i + (j + 1) // LN, (j + 1) % LN)
                    dve.wait_ge(ln_std, t + 1)
                    seq.did(v.reciprocal(std[:, 2 + c:3 + c], std[:, c:c + 1]))
                    seq.wait()
                    if not ln_first(i, j, 2):
                        dve.wait_ge(ln_tr, t - 1)
                    v.tensor_scalar(lnn[c], lnx[j], mv[:, c, 0:1], std[:, 2 + c:3 + c], ALU.subtract, ALU.mult).then_inc(ln_norm, 1)
                    if not ln_first(i, j, 2):
                        ln_scores(t - 2, c)
                seq.end(LT - 2 if inner else 1)

            seq.start(1, 0)
            ln_stats(0, 0, 0)
            seq.end(1)
            ln_run(dve, ln_turn)
            ln_scores(TT - 2, 0)
            ln_scores(TT - 1, 1)
            n_r = [0]

            def did(ins):
                ins.then_inc(r_dve, 1)
                n_r[0] += 1
                dve.wait_ge(r_dve, n_r[0])

            bc = lambda a: a.rearrange("p (a b) -> p a b", b=1).broadcast_to([NA, TT, E])
            dve.wait_ge(r_pe, 1)
            dve.wait_ge(ln_h, TT)
            did(v.tensor_copy(rt(1), ps[6][0:NA, 0:TT * E].rearrange("p (a b) -> p a b", a=TT)))
            dve.wait_ge(r_act, 2)
            v.tensor_reduce(gmx[:, 0:1], rt(2), AX.XY, ALU.max)
            did(v.tensor_reduce(gmx[:, 1:2], rt(3), AX.XY, ALU.max))
            dve.wait_ge(r_pool, 1)
            seq.start(17, 0)
            step = lambda ins: (seq.did(ins), seq.wait())
            step(v.tensor_scalar(gmx[:, 4:6], gmx[:, 2:4], 1e-6, None, ALU.max))
            step(v.reciprocal(gmx[:, 0:2], gmx[:, 4:6]))
            step(v.tensor_scalar(gmx[:, 2:4], gmx[:, 0:2], 0.5, None, ALU.mult))
            step(v.tensor_scalar(rt(0), rt(0), gmx[:, 2:3], None, ALU.mult))
            step(v.tensor_scalar(rt(1), rt(1), gmx[:, 3:4], None, ALU.mult))
            did(v.tensor_tensor(rt(3), rt(1), rt(0), ALU.add))
            step(v.tensor_reduce(r16(0), rt(3), AX.X, ALU.max))
            did(v.tensor_tensor(rt(3), rt(3), bc(r16(0)), ALU.subtract))
            dve.wait_ge(r_act, 3)
            did(v.tensor_reduce(r16(1), rt(2), AX.X, ALU.add))
            step(v.reciprocal(r16(2), r16(1)))
            did(v.tensor_tensor(rt(1), rt(2), bc(r16(2)), ALU.mult))
            for t in range(TT):
                ins = v.max(rt(4)[:, t, :], rt(1)[:, t, :])
            step(ins)
            did(v.tensor_tensor(rt(0), rt(1), rt(4)[:, :, 1:2].broadcast_to([NA, TT, E]), ALU.subtract))
            dve.wait_ge(r_dve, 8)
            step(v.tensor_scalar(rt(3), rt(3), 1.0, None, ALU.add))
            step(v.reciprocal(rt(2), rt(3)))
            step(v.tensor_tensor(rt(0), rt(1), rt(2), ALU.mult))
            step(v.tensor_reduce(r16(3), rt(0), AX.X, ALU.add))
            step(v.tensor_scalar(r16(4), r16(3), 1e-9, None, ALU.add))
            step(v.reciprocal(r16(5), r16(4)))
            step(v.tensor_tensor(rt(5), rt(0), bc(r16(5)), ALU.mult))
            step(v.tensor_copy(gmx[:, 6:7], gmx[:, 4:5]))
            step(v.tensor_copy(gmx[:, 6:7], gmx[:, 4:5]))
            seq.end(1)
            v.tensor_copy(gmx[:, 6:7], gmx[:, 4:5]).then_inc(r_dve, 2)
            dve.wait_ge(r_pe, 3)
            for h in range(2):
                zv = z_t[:, h * L:(h + 1) * L].rearrange("p (a b) -> p a b", b=2)
                pm = ps[2 + h][0:RANK, :].rearrange("p (a b) -> p a b", b=1).broadcast_to([RANK, T, 2])
                ins = v.scalar_tensor_tensor(zv, pm, 0.5, zv, ALU.mult, ALU.mult)
            ins.then_inc(r_zp, 1)

            def dt(c, k, j):
                dve.wait_ge(act_sp, k * 2 + (j + MT * c + 1))
                dve.wait_ge(ld_s[j], (k + (PAIRS * c + 1)) * 32)
                seq.wait()
                seq.did(v.scalar_tensor_tensor(ndt[:], rl[:], -1.0, lg[:], ALU.mult, ALU.subtract))
                seq.wait()
                v.scalar_tensor_tensor(dtu[:], ndt[:], -1.0, ui[:, j, :], ALU.mult, ALU.mult).then_inc(dve_dt, 1)

            def before_s(cs, co):
                if cs == 0:
                    seq.start(1, 0)
                    dt(0, 0, 0)
                    seq.end(1)

            def y_count(c):
                return MT * sum(len(u) for u in PE_UNITS[:c])

            def body(p):
                cx, cs, co = p.cx, p.cs, p.co
                units = PE_UNITS[cs] if cs is not None else ()
                carried = cs is not None and cs % HALVES > 0
                carries = cs is not None and cs % HALVES < HALVES - 1
                mine = [q for q in range(NU) if q not in units]
                per = 0
                if cs is not None:
                    per += 2 * (carried + NU + NU * U + 2 * len(mine) - 1 + 1) + sum(p.next_s(j) is not None for j in range(2))
                if cx is not None:
                    per += 2 * (1 + K_CONV)
                if co is not None:
                    per += 1
                seq.start(per, p.turn)
                for j in range(2):
                    m, ms = p.i * 2 + j, p.k * 2 + j
                    gs = p.s(j) if cs is not None else None
                    gx = p.x(j) if cx is not None else None
                    made, summed = {}, {}

                    def add_pair(q):
                        dve.wait_ge(pool_p, gs * NU + (q + 1))
                        p0, p1 = hb[:, q % RING, 0, :], hb[:, q % RING, 1, :]
                        if q == mine[0] and not p.s_start(j):
                            dve.wait_ge(dve_y, gs)
                        summed[q] = seq.did(v.tensor_tensor(yacc[:] if q == mine[0] else p0, p0, p1, ALU.add))

                    def add_on(q):
                        if q != mine[0]:
                            seq.wait(summed[q])
                            if q == mine[1]:
                                dve.wait_ge(dve_ud, gs + 1)
                            summed[q] = seq.did(v.tensor_tensor(yacc[:], yacc[:], hb[:, q % RING, 0, :], ALU.add))

                    def add_ud():
                        seq.wait(summed[mine[0]])
                        v.scalar_tensor_tensor(yacc[:], ui[:, j, :], ws[:, j, SP_D:SP_D + 1], yacc[:], ALU.mult, ALU.add).then_inc(dve_ud, 1)

                    def make(q):
                        if q - RING in units:
                            dve.wait_ge(pe_y, y_count(cs) + ms * len(units) + (units.index(q - RING) + 1))
                        if p.s_first and j == 0 and q % (NU // PB) == 0:
                            dve.wait_ge(ld_b[q // (NU // PB)], 16 * (cs + 1))
                        if q - RING in summed:
                            seq.wait(summed[q - RING])
                        w = dtu[:].rearrange("p (a t) -> p a t", a=1).broadcast_to([P, U, T])
                        made[q] = seq.did(v.tensor_tensor(hb[:, q % RING], w, bb[:, q * U:(q + 1) * U, :], ALU.mult))

                    tap = lambda k: wxx[:, j, SS + k:SS + k + 1]

                    def conv(k):
                        if k == 0:
                            seq.wait()
                            seq.did(v.tensor_scalar(xc[:], xraw[:, 0:T], tap(0), tap(K_CONV), ALU.mult, ALU.add))
                        else:
                            seq.wait(taps[-1])
                            seq.did(v.scalar_tensor_tensor(xc[:], xraw[:, k:k + T], tap(k), xc[:], ALU.mult, ALU.add))
                        taps.append(seq.n)

                    taps = []
                    if cs is not None:
                        if not p.s_start(j):
                            dve.wait_ge(dve_h, gs * NU)
                        if carried:
                            loaded = seq.did(v.tensor_scalar(st[:], states[:, bass.ds(ms, 1), :].rearrange("p a b -> p (a b)"), 1.0, None, ALU.mult))
                        dve.wait_ge(dve_dt, gs + 1)
                        if not p.s_start(j):
                            dve.wait_ge(dve_y, gs)
                        make(0)
                        for q in range(NU):
                            if q + 1 < NU:
                                make(q + 1)
                            hq = hb[:, q % RING]
                            seq.wait(max(made[q], loaded if carried else 0))
                            dve.wait_ge(act_da, gs * NU + (q + 1))
                            for n in range(U):
                                init = st[:, q * U + n:q * U + n + 1] if carried else 0.0
                                scanned = seq.did(v.tensor_tensor_scan(hq[:, n, :], da[:, q % 2, n, :], hq[:, n, :], init, ALU.mult, ALU.add))
                            if q - 2 in mine:
                                add_pair(q - 2)
                            seq.wait(scanned)
                            v.tensor_copy(st[:, q * U:(q + 1) * U], hq[:, :, T - 1:T].rearrange("p a b -> p (a b)")).then_inc(dve_h, 1)
                            if q - 2 in mine:
                                add_on(q - 2)
                                if q - 2 == mine[0]:
                                    add_ud()
                        if carries:
                            dve.wait_ge(dve_h, gs * NU + NU)
                            v.tensor_scalar(states[:, bass.ds(ms, 1), :].rearrange("p a b -> p (a b)"), st[:], 1.0, None, ALU.mult)
                        if p.next_s(j):
                            dt(*p.next_s(j))
                    if cx is not None:
                        dve.wait_ge(act_x, gx + 1)
                        if not p.start(j):
                            dve.wait_ge(act_u, gx)
                            dve.wait_ge(dve_conv, gx)
                        dve.wait_ge(ld_w[j], (p.i + (PAIRS * cx + 1)) * 16)
                        if cx % HALVES == 0:
                            seq.did(v.memset(xraw[:, 0:HALO], 0.0))
                        else:
                            seq.did(v.tensor_scalar(xraw[:, 0:HALO], tails[:, bass.ds(m, 1), :].rearrange("p a b -> p (a b)"), 1.0, None, ALU.mult))
                        conv(0)
                    if NU - 2 in mine and cs is not None:
                        add_pair(NU - 2)
                    if cx is not None:
                        conv(1)
                    if cs is not None:
                        if NU - 2 in mine:
                            add_on(NU - 2)
                        add_pair(NU - 1)
                    if cx is not None:
                        conv(2)
                    if cs is not None:
                        add_on(NU - 1)
                    if cx is not None:
                        conv(3)
                        seq.wait(taps[-1])
                        v.tensor_scalar(tails[:, bass.ds(m, 1), :].rearrange("p a b -> p (a b)"), xraw[:, T:T + HALO], 1.0, None, ALU.mult).then_inc(dve_conv, 1)
                    if cs is not None:
                        seq.wait(summed[NU - 1])
                        dve.wait_ge(ld_sg[j], (p.k + (PAIRS * cs + 1)) * 16)
                        dve.wait_ge(pe_y, y_count(cs) + (ms + 1) * len(units))
                        seq.did(v.tensor_tensor(yacc[:], yacc[:], p_y[:], ALU.add))
                        seq.wait()
                        v.tensor_tensor(sgi[:, j, :], yacc[:], sgi[:, j, :], ALU.mult).then_inc(dve_y, 1)
                    if co is not None and j == 1:
                        go_n = p.k + OT * co
                        dve.wait_ge(pe_o, (go_n + 1) * 2)
                        dve.wait_ge(ld_r, (go_n + 1) * 32)
                        seq.did(v.tensor_tensor(go[:], p_o[:], go[:], ALU.mult))
                        seq.wait()
                        v.tensor_tensor(xo[:], xo[:], go[:], ALU.add).then_inc(dve_o, 1)
                seq.end(p.turns)

            def after_x(cx):
                dve.wait_ge(act_rms, cx + 1)
                seq.start(1, 0)
                seq.did(v.reciprocal(ssn[cx % 2], ssn[cx % 2]))
                seq.wait()
                v.tensor_tensor(ssn[cx % 2], ssn[cx % 2], ssr, ALU.mult).then_inc(dve_ssn, 1)
                seq.end(1)

            run(dve, body, before_s, after_x)

        @block.gpsimd
        def _(pool):
            pool.wait_ge(r_dve, 2)
            nc.gpsimd.partition_all_reduce(gmx[:, 2:4], gmx[:, 0:2], NA, bass.bass_isa.ReduceOp.max).then_inc(r_pool, 1)

            def body(p):
                for j in range(2 if p.cs is not None else 0):
                    for q in range(NU):
                        if p.s_first and j == 0 and q % (NU // PB) == 0:
                            pool.wait_ge(ld_c[q // (NU // PB)], 16 * (p.cs + 1))
                        pool.wait_ge(dve_h, p.s(j) * NU + (q + 1))
                        nc.gpsimd.tensor_tensor(hb[:, q % RING], hb[:, q % RING], cb[:, q * U:(q + 1) * U, :], ALU.mult).then_inc(pool_p, 1)

            run(pool, body)


_OUTS = ("out", (NC, OT, P, T))


def kernel(L0_attn_hidden_states, L0_attn_W_in, L0_attn_conv_w, L0_attn_conv_b, L0_attn_W_x, L0_attn_W_dt,
           L0_attn_b_dt, L0_attn_A_log, L0_attn_D, L0_attn_W_out, L0_ffn_W, L0_ffn_b, L0_ffn_A, L0_ffn_Bmat,
           L0_ffn_LiMEs):
    import numpy as np
    import concourse.bacc as bacc
    from concourse.bass_utils import run_bass_kernel_spmd

    def tiles(w, k):
        return w.reshape(-1, P, k, P).transpose(0, 3, 2, 1).reshape(-1, P, k * P)

    def cols(v):
        return v.reshape(-1, P, v.size // v.shape[0])

    x = L0_attn_hidden_states.reshape(TOK, H)
    f32 = x.dtype
    w_in = tiles(L0_attn_W_in, KH)
    w_dt = np.zeros((MT, P, P), f32)
    w_dt[:, :R] = L0_attn_W_dt.reshape(MT, P, R).transpose(0, 2, 1)
    b_mat = np.zeros((OT, P, P), f32)
    b_mat[:, SS:] = L0_ffn_Bmat.reshape(RANK, OT, P).transpose(1, 0, 2)
    blk = np.zeros((SS, SS), f32)
    for a, n in ((0, R), (R, N), (R + N, N)):
        blk[a:a + n, a:a + n] = 1.0 / n
    arrays = {
        "x": x.reshape(TT, P, H),
        "xt": x.reshape(NC, T, OT, P).transpose(0, 2, 3, 1),
        "w_in": w_in[:MT],
        "w_x": np.concatenate([L0_attn_W_x.T.reshape(MT, P, SS), cols(L0_attn_conv_w),
                               cols(L0_attn_conv_b)], axis=2),
        "w_s": np.concatenate([cols(L0_attn_A_log), cols(L0_attn_b_dt), cols(L0_attn_D), w_dt], axis=2),
        "w_g": w_in[MT:],
        "w_o": tiles(L0_attn_W_out, MT),
        "w_f": np.concatenate([tiles(L0_ffn_W, KH), b_mat, cols(L0_ffn_b)], axis=2),
        "w8": L0_ffn_W[:E].reshape(E, KH, P).transpose(2, 1, 0),
        "a_r": L0_ffn_A.reshape(KH, P, RANK).transpose(1, 0, 2),
        "lime": L0_ffn_LiMEs,
        "lime_t": L0_ffn_LiMEs.T,
        "b8": np.broadcast_to(L0_ffn_b[:E], (NA, E)),
        "ident": np.eye(P, dtype=f32),
        "blk": blk,
    }
    nc = bacc.Bacc("TRN2", target_bir_lowering=False, num_devices=1)
    arrays = {k: np.ascontiguousarray(v) for k, v in arrays.items()}
    args = [nc.dram_tensor(k, v.shape, F32, kind="ExternalInput").ap() for k, v in arrays.items()]
    out = nc.dram_tensor(_OUTS[0], _OUTS[1], F32, kind="ExternalOutput").ap()
    build(nc, *args, out)
    r = run_bass_kernel_spmd(nc, [arrays], core_ids=[0]).results[0]["out"]
    return r.transpose(0, 3, 1, 2).reshape(BATCH, L, H)
```
